# Optimizing a Trainium2 kernel written in Bass

```python
import numpy as np
import jax
import jax.numpy as jnp

def _softmax(x, axis=-1):
    return jax.nn.softmax(x, axis=axis)

def _gelu(x):
    return jax.nn.gelu(x, approximate=True)

def _silu(x):
    return jax.nn.silu(x)

def _sigmoid(x):
    return jax.nn.sigmoid(x)

def _layernorm(x, axis=-1, eps=1e-05):
    m = jnp.mean(x, axis=axis, keepdims=True)
    v = jnp.var(x, axis=axis, keepdims=True)
    return (x - m) / jnp.sqrt(v + eps)

def _scatter_add(tgt, idx, src, axis=0):
    return tgt.at[idx].add(src)

def _segment_sum(src, seg, n):
    return jax.ops.segment_sum(src, seg, n)
kernel_name = 'mk_gnn_resnorm_d2_gnn_r8_f2a292'

def setup_inputs(seed: int=0):
    np.random.seed(seed)
    _w = jnp.asarray

    def _rec_inputs():
        import jax
        import jax.numpy as jnp
        _gk = jax.random.key(seed)
        x = -0.000202 + 1 * jax.random.normal(jax.random.fold_in(_gk, 1), (6250, 128), jnp.float32)
        src = jax.random.randint(jax.random.fold_in(_gk, 2), (200000,), 0, 6250, jnp.int32)
        dst = jax.random.randint(jax.random.fold_in(_gk, 3), (200000,), 0, 6250, jnp.int32)
        _o = jnp.argsort(dst, stable=True)
        src = src[_o]
        dst = dst[_o]
        edge_attr_16 = 0.000254156 + 0.999948 * jax.random.normal(jax.random.fold_in(_gk, 12), (200000, 16), jnp.float32)
        return (x, src, dst, edge_attr_16)
    x, src, dst, edge_attr_16 = _rec_inputs()

    def _L0_gnn_setup():
        import jax, jax.numpy as jnp
        import numpy as np
        N_NODES = 6250
        N_EDGES = 100000
        HIDDEN = 128
        EDGE_FEAT = 16
        N_LAYERS = 3
        key = jax.random.key(seed)
        ks = jax.random.split(key, 8)
        s1 = 1.0 / np.sqrt(HIDDEN + EDGE_FEAT)
        s2 = 1.0 / np.sqrt(HIDDEN)
        return {'x': jax.random.normal(ks[0], (N_NODES, HIDDEN), jnp.float32), 'edge_index': jax.random.randint(ks[1], (2, N_EDGES), 0, N_NODES, jnp.int32), 'edge_attr': jax.random.normal(ks[2], (N_EDGES, EDGE_FEAT), jnp.float32), 'W1': jax.random.normal(ks[3], (N_LAYERS, HIDDEN + EDGE_FEAT, HIDDEN), jnp.float32) * s1, 'b1': jnp.zeros((N_LAYERS, HIDDEN), jnp.float32), 'W2': jax.random.normal(ks[4], (N_LAYERS, HIDDEN, HIDDEN), jnp.float32) * s2, 'b2': jnp.zeros((N_LAYERS, HIDDEN), jnp.float32), 'Wself': jax.random.normal(ks[5], (N_LAYERS, HIDDEN, HIDDEN), jnp.float32) * s2, 'bself': jnp.zeros((N_LAYERS, HIDDEN), jnp.float32)}
    _L0_gnn_all = _L0_gnn_setup()
    _L0_gnn_in = {k: v for k, v in _L0_gnn_all.items() if k in ('W1', 'b1', 'W2', 'b2', 'Wself', 'bself')}
    del _L0_gnn_all

    def _L1_gnn_setup():
        import jax, jax.numpy as jnp
        import numpy as np
        N_NODES = 6250
        N_EDGES = 100000
        DIM = 128
        key = jax.random.key(seed)
        ks = jax.random.split(key, 8)
        scale = 1.0 / np.sqrt(DIM)
        z = jax.random.normal(ks[0], (N_NODES, DIM), dtype=jnp.float32)
        Wq = jax.random.normal(ks[1], (DIM, DIM), dtype=jnp.float32) * scale
        Wk = jax.random.normal(ks[2], (DIM, DIM), dtype=jnp.float32) * scale
        Wv = jax.random.normal(ks[3], (DIM, DIM), dtype=jnp.float32) * scale
        bq = jnp.zeros((DIM,), dtype=jnp.float32)
        bk = jnp.zeros((DIM,), dtype=jnp.float32)
        bv = jnp.zeros((DIM,), dtype=jnp.float32)
        src = jax.random.randint(ks[4], (N_EDGES,), 0, N_NODES, dtype=jnp.int32)
        dst = jax.random.randint(ks[5], (N_EDGES,), 0, N_NODES, dtype=jnp.int32)
        return {'z': z, 'Wq': Wq, 'bq': bq, 'Wk': Wk, 'bk': bk, 'Wv': Wv, 'bv': bv, 'src': src, 'dst': dst}
    _L1_gnn_all = _L1_gnn_setup()
    _L1_gnn_in = {k: v for k, v in _L1_gnn_all.items() if k in ('Wq', 'bq', 'Wk', 'bk', 'Wv', 'bv')}
    del _L1_gnn_all
    return {'x': x, 'src': src, 'dst': dst, 'edge_attr_16': edge_attr_16, 'L0_gnn_W1': _L0_gnn_in['W1'], 'L0_gnn_b1': _L0_gnn_in['b1'], 'L0_gnn_W2': _L0_gnn_in['W2'], 'L0_gnn_b2': _L0_gnn_in['b2'], 'L0_gnn_Wself': _L0_gnn_in['Wself'], 'L0_gnn_bself': _L0_gnn_in['bself'], 'L1_gnn_Wq': _L1_gnn_in['Wq'], 'L1_gnn_bq': _L1_gnn_in['bq'], 'L1_gnn_Wk': _L1_gnn_in['Wk'], 'L1_gnn_bk': _L1_gnn_in['bk'], 'L1_gnn_Wv': _L1_gnn_in['Wv'], 'L1_gnn_bv': _L1_gnn_in['bv']}

def reference(x, src, dst, edge_attr_16, L0_gnn_W1, L0_gnn_b1, L0_gnn_W2, L0_gnn_b2, L0_gnn_Wself, L0_gnn_bself, L1_gnn_Wq, L1_gnn_bq, L1_gnn_Wk, L1_gnn_bk, L1_gnn_Wv, L1_gnn_bv):
    import jax
    import jax.numpy as jnp

    def _L0_gnn_ref(x, edge_index, edge_attr, W1, b1, W2, b2, Wself, bself):
        import jax, jax.numpy as jnp
        import numpy as np
        N_NODES = 6250
        N_EDGES = 100000
        HIDDEN = 128
        EDGE_FEAT = 16
        N_LAYERS = 3
        src = edge_index[0]
        dst = edge_index[1]
        n = x.shape[0]
        ones = jnp.ones((src.shape[0], 1), x.dtype)
        cnt = jax.ops.segment_sum(ones, dst, num_segments=n)
        denom = jnp.maximum(cnt, 1.0)
        for l in range(W1.shape[0]):
            msg_in = jnp.concatenate([x[src], edge_attr], axis=1)
            h = jax.nn.relu(msg_in @ W1[l] + b1[l]) @ W2[l] + b2[l]
            aggr = jax.ops.segment_sum(h, dst, num_segments=n) / denom
            x = x @ Wself[l] + bself[l] + aggr
        return x

    def _L1_gnn_ref(z, Wq, bq, Wk, bk, Wv, bv, src, dst):
        import jax, jax.numpy as jnp
        import numpy as np
        N_NODES = 6250
        N_EDGES = 100000
        DIM = 128
        tau = 1.0 / np.sqrt(z.shape[-1] * 1.0)
        n = z.shape[0]
        q = z @ Wq + bq
        k = z @ Wk + bk
        v = z @ Wv + bv
        e = jnp.einsum('ed,ed->e', k[src], q[dst]) * jnp.asarray(tau, z.dtype)
        m = jax.ops.segment_max(e, dst, num_segments=n)
        m = jnp.where(jnp.isfinite(m), m, jnp.zeros_like(m))
        ex = jnp.exp(e - m[dst])
        denom = jax.ops.segment_sum(ex, dst, num_segments=n)
        num = jax.ops.segment_sum(ex[:, None] * v[src], dst, num_segments=n)
        h = num / jnp.where(denom > 0, denom, jnp.ones_like(denom))[:, None]
        return h
    edge_index = jnp.stack([src, dst])
    x = _layernorm(x + _L0_gnn_ref(x, edge_index, edge_attr_16, L0_gnn_W1, L0_gnn_b1, L0_gnn_W2, L0_gnn_b2, L0_gnn_Wself, L0_gnn_bself), axis=-1)
    x = _layernorm(x + _L1_gnn_ref(x, L1_gnn_Wq, L1_gnn_bq, L1_gnn_Wk, L1_gnn_bk, L1_gnn_Wv, L1_gnn_bv, src, dst), axis=-1)
    return x

_drawn_inputs = setup_inputs


def setup_inputs(seed=0):
    import zlib

    import numpy as np

    out = dict(_drawn_inputs(seed))
    spreads = {'L0_gnn_b1': (0.0, 0.1),
     'L0_gnn_b2': (0.0, 0.1),
     'L0_gnn_bself': (0.0, 0.1),
     'L1_gnn_bq': (0.0, 0.563),
     'L1_gnn_bk': (0.0, 0.8),
     'L1_gnn_bv': (0.0, 0.1)}
    factors = {}
    for name, (base, spread) in spreads.items():
        noise = np.random.default_rng([zlib.crc32(name.encode()), seed]).standard_normal(out[name].shape)
        drawn = base * np.exp(spread * noise) if base else spread * noise
        out[name] = jnp.asarray(drawn.astype(out[name].dtype))
    for name, factor in factors.items():
        out[name] = (out[name] * factor).astype(out[name].dtype)
    return out
```

```python
from contextlib import ExitStack

import concourse.bass as bass
from concourse import mybir

P = 128
N_NODES, N_EDGES, D, DE, N_LAYERS = 6250, 200000, 128, 16, 3
TILES = 4
GROUP = P * TILES
SLOTS = 4
ROWS = 98
ROUNDS = 4
GROUPS = ROWS * ROUNDS
WIN = 32
CHUNK = 512
CHUNKS = 13
NODES = CHUNK * CHUNKS
NTILES = -(-N_NODES // P)
LAST_ROWS = N_NODES - (NTILES - 1) * P
PAD_DST = N_NODES
EPS = 1e-5
TAU = float(D) ** -0.5
MASKED = -1e30
NO_MAX = -1e20

fp32 = mybir.dt.float32
i32 = mybir.dt.int32
ALU = mybir.AluOpType
ACT = mybir.ActivationFunctionType
AX = mybir.AxisListType


def gnn_attention(nc, x, src, dst, edge_attr, W1, b1, W2, b2, Wself, bself, Wq, bq, Wk, bk, Wv, bv, out):
    ctx = ExitStack()
    with ctx:
        def sb(name, shape, dt=fp32):
            return ctx.enter_context(nc.sbuf_tensor(name, shape, dt))

        def ps(name, shape, dt=fp32):
            return ctx.enter_context(nc.psum_tensor(name, shape, dt))

        def sem(name):
            return ctx.enter_context(nc.semaphore(name))

        gather_rows = nc.dram_tensor("gather_rows", (NODES, D), fp32, kind="Internal").ap()
        kv_rows = nc.dram_tensor("kv_rows", (NODES, 2 * D), fp32, kind="Internal").ap()
        z_rows = nc.dram_tensor("z_rows", (NODES, D), fp32, kind="Internal").ap()
        base_dram = nc.dram_tensor("base_dram", (ROUNDS, ROWS), i32, kind="Internal").ap()

        nodeT = sb("nodeT", [P, NODES])
        acc = sb("acc", [P, 2, NODES])
        maxB = sb("maxB", [P, NODES])
        iotaN = sb("iotaN", [P, NODES])
        dstT = sb("dstT", [P, GROUPS, TILES])
        srcT = sb("srcT", [P, GROUPS, TILES], i32)
        base_row = sb("base_row", [1, GROUPS], i32)
        ident = sb("ident", [P, P])
        ones = sb("ones", [P, P])
        w1x = sb("w1x", [P, D])
        w1e = sb("w1e", [TILES * DE, TILES, D])
        w2 = sb("w2", [P, D])
        wself = sb("wself", [P, D])
        b1_row = sb("b1_row", [1, D])
        b2_row = sb("b2_row", [1, D])
        bself_col = sb("bself_col", [P, 1])
        wq = sb("wq", [P, D])
        wkv = sb("wkv", [P, 2 * D])
        bkv_row = sb("bkv_row", [1, 2 * D])
        bq_col = sb("bq_col", [P, 1])
        idx = [sb(f"idx{s}", [P, TILES], i32) for s in range(SLOTS)]
        attr = sb("attr", [P, SLOTS, TILES * DE])
        attrT = sb("attrT", [TILES * DE, SLOTS, P])
        onehot = sb("onehot", [P, 2, TILES, WIN])
        work = sb("work", [P, SLOTS * TILES * 2 * D])
        msg = work[:, 0:SLOTS * TILES * D].rearrange("p (s j f) -> p s j f", s=SLOTS, j=TILES)
        kv = work[:, :].rearrange("p (s j f) -> p s j f", s=SLOTS, j=TILES)
        natural = work[0:ROWS, 0:ROUNDS * GROUP].rearrange("p (r e) -> p r e", r=ROUNDS)
        natural_i = work[0:ROWS, ROUNDS * GROUP:2 * ROUNDS * GROUP].bitcast(i32).rearrange("p (r e) -> p r e", r=ROUNDS)
        keysT = sb("keysT", [P, 2, TILES * P])
        score = sb("score", [P, 2, TILES, WIN])
        diag = sb("diag", [P, P])
        gmax = sb("gmax", [P, 1])
        gmax4 = sb("gmax4", [P, TILES])
        group_max = sb("group_max", [P, WIN])
        new_max = sb("new_max", [P, WIN])
        decay = sb("decay", [P, WIN])
        rows_in = sb("rows_in", [P, 2, D])
        stage = sb("stage", [P, CHUNK])
        stage2 = sb("stage2", [P, CHUNK])
        ind = sb("ind", [P, CHUNK])
        x_stage = sb("x_stage", [P, CHUNK])
        outside = sb("outside", [P, TILES, WIN])
        group_den = sb("group_den", [P, WIN])
        tau_bq = sb("tau_bq", [P, 1])
        rows_out = sb("rows_out", [P, TILES, D])
        z_out = sb("z_out", [P, D])
        zT = sb("zT", [P, P])
        stats = sb("stats", [P, 6])
        mv = sb("mv", [P, 2])
        std = sb("std", [P, 1])
        rstd = sb("rstd", [P, 1])
        base_i = sb("base_i", [ROWS, ROUNDS], i32)
        eps_col = sb("eps_col", [P, 1])
        far_dst = sb("far_dst", [P, GROUPS, TILES])
        far_i = sb("far_i", [1, 1], i32)
        is_far = work[:, 0:GROUPS * TILES].rearrange("p (g j) -> p g j", g=GROUPS)
        base_all = work[:, GROUPS * TILES:GROUPS * TILES + GROUPS]
        base_all_i = work[:, GROUPS * TILES + GROUPS:GROUPS * TILES + 2 * GROUPS].bitcast(i32)
        wide = sb("wide", [P, TILES, CHUNK])
        zero_col = sb("zero_col", [P, 1])

        psA = ps("psA", [P, 512])
        psB = ps("psB", [P, 512])
        psC = ps("psC", [P, 512])
        psD = ps("psD", [P, 512])
        psE = ps("psE", [P, 512])
        psF = ps("psF", [P, 512])
        psG = ps("psG", [P, 512])
        psH = ps("psH", [P, 512])

        s_w = sem("s_w")
        s_layer_w = sem("s_layer_w")
        s_const = sem("s_const")
        s_attr = [sem(f"s_attr{s}") for s in range(SLOTS)]
        s_gather = [sem(f"s_gather{s}") for s in range(SLOTS)]
        s_idx = sem("s_idx")
        s_pool = sem("s_pool")
        s_slot_free = sem("s_slot_free")
        s_attrT = sem("s_attrT")
        s_attrT_sb = sem("s_attrT_sb")
        s_edge_term = sem("s_edge_term")
        s_pre = sem("s_pre")
        s_relu = sem("s_relu")
        s_onehot = sem("s_onehot")
        s_scatter = sem("s_scatter")
        s_node = {}

        def seq(name):
            if name not in s_node:
                s_node[name] = sem("prep_" + name)
            return s_node[name]

        s_diag = sem("s_diag")
        s_h = sem("s_h")
        s_hT = sem("s_hT")
        s_keysT = sem("s_keysT")
        s_keysT_ps = sem("s_keysT_ps")
        s_kv_ps = sem("s_kv_ps")
        s_kv_sb = sem("s_kv_sb")
        s_kv_st = sem("s_kv_st")
        s_masked = sem("s_masked")
        s_maxB_ps = sem("s_maxB_ps")
        s_mean = sem("s_mean")
        s_mix = sem("s_mix")
        s_nw = sem("s_nw")
        s_o = sem("s_o")
        s_out = sem("s_out")
        s_probs = sem("s_probs")
        s_q_ps = sem("s_q_ps")
        s_rows_ps = sem("s_rows_ps")
        s_rows_sb = sem("s_rows_sb")
        s_rows_st = sem("s_rows_st")
        s_scoreT = sem("s_scoreT")
        s_score_ps = sem("s_score_ps")
        s_shifted = sem("s_shifted")
        s_std = sem("s_std")
        s_var = sem("s_var")
        s_x3 = sem("s_x3")
        s_x_in = sem("s_x_in")
        s_x_ps = sem("s_x_ps")
        s_x_sb = sem("s_x_sb")
        s_xs = sem("s_xs")
        s_z = sem("s_z")
        s_zT = sem("s_zT")
        s_zT_ps = sem("s_zT_ps")
        s_z_in = sem("s_z_in")
        s_z_st = sem("s_z_st")
        s_tau_bq = sem("s_tau_bq")
        f_attr = sem("f_attr")
        f_attrT = sem("f_attrT")
        f_attrT_sb = sem("f_attrT_sb")
        f_gather = sem("f_gather")
        f_idx = sem("f_idx")
        f_onehot = sem("f_onehot")
        f_pre = sem("f_pre")
        f_relu = sem("f_relu")
        f_scatter = sem("f_scatter")
        f_term = sem("f_term")
        h_chain = sem("h_chain")
        h_diag = sem("h_diag")
        h_gather = sem("h_gather")
        h_idx = sem("h_idx")
        h_keysT = sem("h_keysT")
        h_keysT_ps = sem("h_keysT_ps")
        h_masked = sem("h_masked")
        h_max = sem("h_max")
        h_mix = sem("h_mix")
        h_probs = sem("h_probs")
        h_score = sem("h_score")
        h_scoreT = sem("h_scoreT")
        h_shifted = sem("h_shifted")
        s_tick = sem("s_tick")

        def hold(engine, semaphore, value):
            engine.wait_ge(semaphore, value)
            engine.sem_inc(s_tick, 1)

        class Chain:
            def __init__(self, engine, semaphore, before):
                self.engine, self.semaphore, self.count = engine, semaphore, before

            def link(self, instruction, held=False):
                instruction.then_inc(self.semaphore, 1)
                self.count = self.count + 1
                self.engine.wait_ge(self.semaphore, self.count)
                if held:
                    self.engine.sem_inc(s_tick, 1)

        s_node_chain, s_z_chain, s_attn_chain, s_out_chain = sem("s_node_chain"), sem("s_z_chain"), sem("s_attn_chain"), sem("s_out_chain")

        s_load, s_ld2 = sem("s_load"), sem("s_ld2")
        s_nat, s_tp, s_tc = sem("s_nat"), sem("s_tp"), sem("s_tc")
        s_v = sem("s_v")
        psX = [psA, psB]
        FULL = N_EDGES // GROUP - 3 * ROWS
        REST = N_EDGES % GROUP
        with nc.Block() as block:
            @block.sync
            def _(sp):
                for n, table in enumerate((dst, src)):
                    if n:
                        sp.wait_ge(s_nat, 5)
                    else:
                        sp.wait_ge(s_nat, 1)
                    for r in range(ROUNDS - 1):
                        sp.dma_start(natural_i[:, r, :], table[r * ROWS * GROUP:(r + 1) * ROWS * GROUP]
                                     .rearrange("(p e) -> p e", e=GROUP)).then_inc(s_load, 16)
                    o = (ROUNDS - 1) * ROWS * GROUP
                    sp.dma_start(natural_i[0:FULL, 3, :], table[o:o + FULL * GROUP].rearrange("(p e) -> p e", e=GROUP)).then_inc(s_load, 16)
                    sp.dma_start(natural_i[FULL:FULL + 1, 3, 0:REST], table[o + FULL * GROUP:N_EDGES].rearrange("(p e) -> p e", p=1)).then_inc(s_load, 16)
                sp.wait_ge(s_nat, 3)
                with nc.allow_non_contiguous_dma(reason="392 numbers, once"):
                    sp.dma_start(base_dram.rearrange("r p -> p r"), base_i[:, :]).then_inc(s_ld2, 16)
                sp.wait_ge(s_ld2, 16)
                sp.dma_start(base_row[:, :], base_dram.rearrange("(a r) p -> a (r p)", a=1)).then_inc(s_ld2, 16)
                sp.wait_ge(s_ld2, 32)

            @block.scalar
            def _(act):
                act.dma_start(wq[:, :], Wq).then_inc(s_w, 16)
                act.dma_start(wkv[:, 0:D], Wk).then_inc(s_w, 16)
                act.dma_start(wkv[:, D:2 * D], Wv).then_inc(s_w, 16)
                act.dma_start(bkv_row[:, 0:D], bk.rearrange("(a f) -> a f", a=1)).then_inc(s_w, 16)
                act.dma_start(bkv_row[:, D:2 * D], bv.rearrange("(a f) -> a f", a=1)).then_inc(s_w, 16)
                act.dma_start(bq_col[:, :], bq.rearrange("(p a) -> p a", a=1)).then_inc(s_w, 16)
                act.wait_ge(s_w, 96)

            @block.gpsimd
            def _(pool):
                pool.memset(ident[:, :], 0.0).then_inc(s_const, 1)
                pool.memset(ones[:, :], 1.0)
                pool.wait_ge(s_const, 1)
                pool.affine_select(out=ident[:, :], in_=ident[:, :], compare_op=ALU.not_equal, fill=1.0, base=0,
                                   pattern=[[-1, P]], channel_multiplier=1).then_inc(s_const, 1)
                pool.iota(iotaN[:, :], pattern=[[1, NODES]], base=0, channel_multiplier=0,
                          allow_small_or_imprecise_dtypes=True).then_inc(s_const, 1)
                pool.memset(w1e[:, :, :], 0.0)
                pool.memset(attr[:, :, :], 0.0).then_inc(s_const, 1)

            @block.vector
            def _(dve):
                dve.sem_inc(s_slot_free, SLOTS)
                dve.sem_inc(f_scatter, 1)
                dve.sem_inc(h_mix, 1)
                nc.vector.memset(eps_col[:, :], EPS)
                nc.vector.memset(zero_col[:, :], 0.0)
                nc.vector.memset(nodeT[:, :], 0.0)
                nc.vector.memset(acc[:, :, :], 0.0)
                nc.vector.memset(natural_i[:, 3, :], PAD_DST).then_inc(s_nat, 1)
                dve.wait_ge(s_load, 80)
                nc.vector.tensor_copy(natural[:, :, :], natural_i[:, :, :]).then_inc(s_nat, 1)
                dve.wait_ge(s_nat, 2)
                nc.vector.tensor_reduce(base_i[:, :], natural[:, :, :], AX.X, ALU.min).then_inc(s_nat, 1)
                for n in range(2):
                    for t in range(16):
                        r, j = t // 4, t % 4
                        dve.wait_ge(s_tp, 16 * n + t + 1)
                        table = srcT if n else dstT
                        nc.vector.tensor_copy(table[:, r * ROWS:(r + 1) * ROWS, j], psX[t % 2][:, 0:ROWS]).then_inc(s_tc, 1)
                    if n == 0:
                        nc.vector.memset(natural_i[:, 3, :], 0).then_inc(s_nat, 1)
                        dve.wait_ge(s_nat, 4)
                        dve.wait_ge(s_tp, 16)
                        dve.sem_inc(s_nat, 1)
                        dve.wait_ge(s_load, 160)
                        nc.vector.tensor_copy(natural[:, :, :], natural_i[:, :, :]).then_inc(s_nat, 1)

            @block.tensor
            def _(pe):
                pe.wait_ge(s_const, 2)
                for n in range(2):
                    pe.wait_ge(s_nat, 6 if n else 2)
                    for t in range(16):
                        r, j = t // 4, t % 4
                        if 16 * n + t >= 2:
                            pe.wait_ge(s_tc, 16 * n + t - 1)
                        nc.tensor.transpose(psX[t % 2][:, 0:ROWS], natural[:, r, j:GROUP:TILES], ident[0:ROWS, 0:ROWS]).then_inc(s_tp, 1)

        s_base, s_far_chain, s_far = sem("s_base"), sem("s_far_chain"), sem("s_far")
        with nc.Block() as block:
            @block.sync
            def _(sp):
                sp.dma_start(base_all_i[:, :], base_dram.rearrange("(a r) p -> a (r p)", a=1).to_broadcast([P, GROUPS])).then_inc(s_base, 16)

            @block.vector
            def _(dve):
                chain = Chain(dve, s_far_chain, 0)
                dve.wait_ge(s_base, 16)
                chain.link(nc.vector.tensor_copy(base_all[:, :], base_all_i[:, :]))
                chain.link(nc.vector.tensor_tensor(far_dst[:, :, :], dstT[:, :, :], base_all[:, :].unsqueeze(2).to_broadcast([P, GROUPS, TILES]), ALU.subtract))
                chain.link(nc.vector.tensor_scalar(is_far, far_dst[:, :, :], float(WIN), None, ALU.is_ge))
                chain.link(nc.vector.scalar_tensor_tensor(far_dst[:, :, :], dstT[:, :, :], 1.0, is_far, ALU.add, ALU.mult))
                chain.link(nc.vector.tensor_scalar(far_dst[:, :, :], far_dst[:, :, :], -1.0, None, ALU.add))
                chain.link(nc.vector.tensor_reduce(gmax[:, :], far_dst[:, :, :].rearrange("p g j -> p (g j)"), AX.X, ALU.max))
                chain.link(nc.vector.tensor_scalar(diag[:, :], ident[:, :], gmax[:, :], None, ALU.mult))
                dve.wait_ge(s_far, 1)
                chain.link(nc.vector.tensor_reduce(gmax[0:1, :], psA[0:1, 0:P], AX.X, ALU.max))
                chain.link(nc.vector.tensor_scalar(gmax[0:1, :], gmax[0:1, :], 0.0, None, ALU.is_ge))
                chain.link(nc.vector.tensor_copy(far_i[:, :], gmax[0:1, :]))

            @block.tensor
            def _(pe):
                pe.wait_ge(s_far_chain, 7)
                nc.tensor.matmul(psA[:, 0:P], ones[:, :], diag[:, :], start=True, stop=True).then_inc(s_far, 1)

        far = nc.values_load(far_i[0:1, 0:1], min_val=0, max_val=1)

        s_wl = sem("s_wl")
        with nc.Block() as block:
            @block.sync
            def _(sp):
                sp.dma_start(w1x[:, :], W1[0, 0:D, :]).then_inc(s_wl, 16)
                sp.dma_start(b1_row[:, :], b1[0:1, :]).then_inc(s_wl, 16)
                s = seq("x_in")
                def load(t, rows):
                    sp.wait_ge(seq("xT_ps"), t)
                    sp.dma_start(rows_in[0:rows, 0, :], x[bass.ds(t * P, rows), :]).then_inc(s, 16)
                sp.dma_start(rows_in[:, 0, :], x[0:P, :]).then_inc(s, 16)
                with sp.Fori(1, NTILES - 1) as t:
                    load(t, P)
                load(NTILES - 1, LAST_ROWS)

            @block.tensor
            def _(pe):
                pe.wait_ge(s_wl, 32)
                def tile(t, rows):
                    pe.wait_ge(seq("x_in"), (t + 1) * 16)
                    nc.tensor.transpose(psA[:, 0:rows], rows_in[0:rows, 0, :], ident[0:rows, 0:rows]).then_inc(seq("xT_ps"), 1)
                    pe.wait_ge(s_v, t + 1)
                    nc.tensor.matmul(psB[0:rows, 0:D], stage[:, 0:rows], w1x[:, :], start=True, stop=False)
                    nc.tensor.matmul(psB[0:rows, 0:D], ones[0:1, 0:rows], b1_row[:, :], start=False, stop=True).then_inc(seq("row0_ps"), 1)
                with pe.Fori(0, NTILES - 1) as t:
                    tile(t, P)
                tile(NTILES - 1, LAST_ROWS)

            @block.vector
            def _(dve):
                def tile(t, rows):
                    dve.wait_ge(seq("xT_ps"), t + 1)
                    nc.vector.tensor_copy(stage[:, 0:rows], psA[:, 0:rows])
                    nc.vector.tensor_copy(nodeT[:, bass.ds(t * P, rows)], psA[:, 0:rows]).then_inc(s_v, 1)
                    dve.wait_ge(seq("row0_ps"), t + 1)
                    nc.vector.tensor_copy(rows_out[0:rows, 0, :], psB[0:rows, 0:D]).then_inc(seq("row0_sb"), 1)
                    dve.wait_ge(seq("row0_st"), (t + 1) * 16)
                with dve.Fori(0, NTILES - 1) as t:
                    tile(t, P)
                tile(NTILES - 1, LAST_ROWS)

            @block.scalar
            def _(act):
                def tile(t, rows):
                    act.wait_ge(seq("row0_sb"), t + 1)
                    act.dma_start(gather_rows[bass.ds(t * P, rows), :], rows_out[0:rows, 0, :]).then_inc(seq("row0_st"), 16)
                with act.Fori(0, NTILES - 1) as t:
                    tile(t, P)
                tile(NTILES - 1, LAST_ROWS)
                act.wait_ge(seq("row0_st"), NTILES * 16)

        ITERS = GROUPS // SLOTS
        with nc.Fori(0, N_LAYERS) as layer:
            with nc.Block() as block:
                @block.sync
                def _(sp):
                    for j in range(TILES):
                        sp.dma_start(w1e[DE * j:DE * (j + 1), j, :], W1[bass.ds(layer, 1), D:D + DE, :].rearrange("a k f -> (a k) f")).then_inc(s_layer_w, 16)
                    def load(g, u, start, edges=GROUP):
                        sp.wait_ge(s_slot_free, layer * GROUPS + g + 1)
                        sp.dma_start(attr[0:edges // TILES, u, :],
                                     edge_attr[bass.ds(start, edges), :].rearrange("(p j) k -> p (j k)", j=TILES)).then_inc(s_attr[u], 16)
                    with sp.Fori(0, ITERS - 1) as it:
                        for u in range(SLOTS):
                            load(it * SLOTS + u, u, (it * SLOTS + u) * GROUP)
                    g = GROUPS - SLOTS
                    load(g, 0, g * GROUP)
                    load(g + 1, 1, (g + 1) * GROUP)
                    load(g + 2, 2, (g + 2) * GROUP, REST)
                    load(g + 3, 3, N_EDGES - GROUP)
                    hold(sp, s_layer_w, (layer + 1) * 64)

                @block.gpsimd
                def _(pool):
                    with pool.Fori(0, ITERS) as it:
                        for u in range(SLOTS):
                            n = layer * GROUPS + it * SLOTS + u + 1
                            hold(pool, s_idx, n)
                            for j in range(TILES):
                                nc.gpsimd.indirect_dma_start(msg[:, u, j, :], None, gather_rows[0:N_NODES, :],
                                                             bass.IndirectOffsetOnAxis(ap=idx[u][:, j:j + 1], axis=0)).then_inc(s_gather[u], 16)

                @block.scalar
                def _(act):
                    def copy_idx(g, u):
                        hold(act, s_slot_free, layer * GROUPS + g + 1)
                        nc.scalar.activation(idx[u][:, :], srcT[:, bass.ds(g, 1), :].rearrange("p a j -> p (a j)"), ACT.Copy).then_inc(s_idx, 1)
                    def attr_copy(g, u):
                        act.wait_ge(s_attrT, layer * GROUPS + g + 1)
                        nc.scalar.activation(attrT[:, u, :], (psC, psD)[u % 2][0:TILES * DE, 0:P], ACT.Copy).then_inc(s_attrT_sb, 1)
                    def relu(g, u):
                        act.wait_ge(s_pre, layer * GROUPS + g + 1)
                        nc.scalar.activation(msg[:, u, :, :], msg[:, u, :, :], ACT.Relu).then_inc(s_relu, 1)
                    for u in range(SLOTS - 1):
                        copy_idx(u, u)
                    attr_copy(0, 0)
                    attr_copy(1, 1)
                    with act.Fori(0, ITERS - 1) as it:
                        for u in range(SLOTS):
                            g = it * SLOTS + u
                            attr_copy(g + 2, (u + 2) % SLOTS)
                            relu(g, u)
                            copy_idx(g + SLOTS - 1, (u + SLOTS - 1) % SLOTS)
                    for u in range(SLOTS):
                        g = GROUPS - SLOTS + u
                        if u + 2 < SLOTS:
                            attr_copy(g + 2, u + 2)
                        relu(g, u)
                        if u == 0:
                            copy_idx(g + SLOTS - 1, SLOTS - 1)

                @block.tensor
                def _(pe):
                    def attr_transpose(g, u, it):
                        hold(pe, s_attr[u], (layer * ITERS + it + 1) * 16)
                        nc.tensor.transpose((psC, psD)[u % 2][0:TILES * DE, 0:P], attr[:, u, :], ident[:, :]).then_inc(s_attrT, 1)
                    def edge_term(g, u):
                        pe.wait_ge(s_attrT_sb, layer * GROUPS + g + 1)
                        nc.tensor.matmul((psA, psB)[u % 2][:, :], attrT[:, u, :], w1e[:, :, :].rearrange("p j f -> p (j f)"),
                                         start=True, stop=True).then_inc(s_edge_term, 1)
                    def scatter(g, u):
                        n = layer * GROUPS + g + 1
                        pe.wait_ge(s_onehot, n)
                        for j in range(TILES):
                            nc.tensor.matmul((psE, psF)[u % 2][:, WIN:2 * WIN], ones[:, :], onehot[:, u % 2, j, :], start=(j == 0), stop=(j == TILES - 1))
                        pe.wait_ge(s_relu, n)
                        for j in range(TILES):
                            last = nc.tensor.matmul((psE, psF)[u % 2][:, 0:WIN], msg[:, u, j, :], onehot[:, u % 2, j, :], start=(j == 0), stop=(j == TILES - 1))
                        last.then_inc(s_scatter, 1)
                    pe.wait_ge(s_layer_w, (layer + 1) * 64)
                    attr_transpose(0, 0, 0)
                    attr_transpose(1, 1, 0)
                    edge_term(0, 0)
                    with pe.Fori(0, ITERS - 1) as it:
                        for u in range(SLOTS):
                            g = it * SLOTS + u
                            edge_term(g + 1, (u + 1) % SLOTS)
                            attr_transpose(g + 2, (u + 2) % SLOTS, it + (u + 2) // SLOTS)
                            scatter(g, u)
                    for u in range(SLOTS):
                        g = GROUPS - SLOTS + u
                        if u + 1 < SLOTS:
                            edge_term(g + 1, u + 1)
                        if u + 2 < SLOTS:
                            attr_transpose(g + 2, u + 2, ITERS - 1)
                        scatter(g, u)

                @block.vector
                def _(dve):
                    regs = [nc.vector.alloc_register(f"base{u}") for u in range(SLOTS)]
                    with dve.Fori(0, ITERS) as it:
                        nc.vector.load(regs, base_row[0:1, bass.ds(it * SLOTS, SLOTS)])
                        bases = [nc.vector.snap(r, min_val=0, max_val=PAD_DST) for r in regs]
                        def make_onehot(u):
                            nc.vector.tensor_tensor(onehot[:, u % 2, :, :],
                                                    iotaN[:, bass.ds(bases[u], WIN)].unsqueeze(1).to_broadcast([P, TILES, WIN]),
                                                    dstT[:, bass.ds(it * SLOTS + u, 1), :].rearrange("p a j -> p j a").to_broadcast([P, TILES, WIN]),
                                                    ALU.is_equal).then_inc(s_onehot, 1)
                        make_onehot(0)
                        for u in range(SLOTS):
                            n = layer * GROUPS + it * SLOTS + u + 1
                            dve.wait_ge(s_gather[u], (layer * ITERS + it + 1) * 64)
                            dve.wait_ge(s_edge_term, n)
                            m = msg[:, u, :, :].rearrange("p j f -> p (j f)")
                            nc.vector.tensor_tensor(m, (psA, psB)[u % 2][:, :], m, ALU.add).then_inc(s_pre, 1)
                            if u + 1 < SLOTS:
                                make_onehot(u + 1)
                            dve.wait_ge(s_scatter, n)
                            a = acc[:, :, bass.ds(bases[u], WIN)]
                            nc.vector.tensor_tensor(a, a, (psE, psF)[u % 2][:, 0:2 * WIN].rearrange("p (c w) -> p c w", c=2),
                                                    ALU.add).then_inc(s_slot_free, 1)

            with nc.If(far > 0):
                with nc.Block() as block:
                    @block.sync
                    def _(sp):
                        def load(n, start, edges=GROUP):
                            sp.wait_ge(f_scatter, (layer * GROUPS + n) * CHUNKS + 1)
                            sp.dma_start(attr[0:edges // TILES, 0, :], edge_attr[bass.ds(start, edges), :].rearrange("(p j) k -> p (j k)", j=TILES)).then_inc(f_attr, 16)
                        with sp.Fori(0, GROUPS - 2) as g:
                            load(g, g * GROUP)
                        load(GROUPS - 2, (GROUPS - 2) * GROUP, REST)
                        load(GROUPS - 1, N_EDGES - GROUP)

                    @block.gpsimd
                    def _(pool):
                        with pool.Fori(0, GROUPS) as g:
                            hold(pool, f_idx, layer * GROUPS + g + 1)
                            for j in range(TILES):
                                nc.gpsimd.indirect_dma_start(msg[:, 0, j, :], None, gather_rows[0:N_NODES, :],
                                                             bass.IndirectOffsetOnAxis(ap=idx[0][:, j:j + 1], axis=0)).then_inc(f_gather, 16)

                    @block.scalar
                    def _(act):
                        with act.Fori(0, GROUPS) as g:
                            n = layer * GROUPS + g + 1
                            hold(act, f_scatter, (n - 1) * CHUNKS + 1)
                            nc.scalar.activation(idx[0][:, :], srcT[:, bass.ds(g, 1), :].rearrange("p a j -> p (a j)"), ACT.Copy).then_inc(f_idx, 1)
                            act.wait_ge(f_attrT, n)
                            nc.scalar.activation(attrT[:, 0, :], psC[0:TILES * DE, 0:P], ACT.Copy).then_inc(f_attrT_sb, 1)
                            act.wait_ge(f_pre, n)
                            nc.scalar.activation(msg[:, 0, :, :], msg[:, 0, :, :], ACT.Relu).then_inc(f_relu, 1)

                    @block.tensor
                    def _(pe):
                        with pe.Fori(0, GROUPS) as g:
                            n = layer * GROUPS + g + 1
                            hold(pe, f_attr, n * 16)
                            nc.tensor.transpose(psC[0:TILES * DE, 0:P], attr[:, 0, :], ident[:, :]).then_inc(f_attrT, 1)
                            pe.wait_ge(f_attrT_sb, n)
                            nc.tensor.matmul(psA[:, :], attrT[:, 0, :], w1e[:, :, :].rearrange("p j f -> p (j f)"), start=True, stop=True).then_inc(f_term, 1)
                            hold(pe, f_relu, n)
                            with pe.Fori(0, CHUNKS) as c:
                                hold(pe, f_onehot, (n - 1) * CHUNKS + c + 1)
                                for j in range(TILES):
                                    nc.tensor.matmul(psE[:, :], msg[:, 0, j, :], wide[:, j, :], start=(j == 0), stop=(j == TILES - 1))
                                for j in range(TILES):
                                    last = nc.tensor.matmul(psF[:, :], ones[:, :], wide[:, j, :], start=(j == 0), stop=(j == TILES - 1))
                                last.then_inc(f_scatter, 1)

                    @block.vector
                    def _(dve):
                        with dve.Fori(0, GROUPS) as g:
                            n = layer * GROUPS + g + 1
                            dve.wait_ge(f_gather, n * 64)
                            dve.wait_ge(f_term, n)
                            m = msg[:, 0, :, :].rearrange("p j f -> p (j f)")
                            nc.vector.tensor_tensor(m, psA[:, :], m, ALU.add).then_inc(f_pre, 1)
                            with dve.Fori(0, CHUNKS) as c:
                                nc.vector.tensor_tensor(wide[:, :, :],
                                                        iotaN[:, bass.ds(c * CHUNK, CHUNK)].unsqueeze(1).to_broadcast([P, TILES, CHUNK]),
                                                        far_dst[:, bass.ds(g, 1), :].rearrange("p a j -> p j a").to_broadcast([P, TILES, CHUNK]),
                                                        ALU.is_equal).then_inc(f_onehot, 1)
                                hold(dve, f_scatter, (n - 1) * CHUNKS + c + 2)
                                a0, a1 = acc[:, 0, bass.ds(c * CHUNK, CHUNK)], acc[:, 1, bass.ds(c * CHUNK, CHUNK)]
                                nc.vector.tensor_tensor(a0, a0, psE[:, :], ALU.add)
                                nc.vector.tensor_tensor(a1, a1, psF[:, :], ALU.add)

            with nc.Block() as block:
                @block.sync
                def _(sp):
                    sp.dma_start(w2[:, :], W2[bass.ds(layer, 1), :, :].rearrange("a k f -> (a k) f")).then_inc(s_nw, 16)
                    sp.dma_start(wself[:, :], Wself[bass.ds(layer, 1), :, :].rearrange("a k f -> (a k) f")).then_inc(s_nw, 16)
                    sp.dma_start(b2_row[:, :], b2[bass.ds(layer, 1), :]).then_inc(s_nw, 16)
                    sp.dma_start(bself_col[:, :], bself[bass.ds(layer, 1), :].rearrange("a (p b) -> (a p) b", b=1)).then_inc(s_nw, 16)
                    nxt = (layer + 1) % N_LAYERS
                    sp.dma_start(w1x[:, :], W1[bass.ds(nxt, 1), 0:D, :].rearrange("a k f -> (a k) f")).then_inc(s_nw, 16)
                    sp.dma_start(b1_row[:, :], b1[bass.ds(nxt, 1), :]).then_inc(s_nw, 16)
                    hold(sp, s_nw, (layer + 1) * 96)
                    with sp.Fori(0, CHUNKS) as c:
                        sp.wait_ge(s_rows_sb, layer * CHUNKS + c + 1)
                        sp.dma_start(gather_rows[bass.ds(c * CHUNK, CHUNK), :].rearrange("(s p) f -> p s f", p=P), rows_out[:, :, :]).then_inc(s_rows_st, 16)
                    hold(sp, s_rows_st, (layer + 1) * CHUNKS * 16)

                @block.vector
                def _(dve):
                    with dve.Fori(0, CHUNKS) as c:
                        n = layer * CHUNKS + c + 1
                        total, count = acc[:, 0, bass.ds(c * CHUNK, CHUNK)], acc[:, 1, bass.ds(c * CHUNK, CHUNK)]
                        chain = Chain(dve, s_node_chain, (n - 1) * 2)
                        chain.link(nc.vector.tensor_scalar(stage2[:, :], count, 1.0, None, ALU.max))
                        chain.link(nc.vector.reciprocal(stage2[:, :], stage2[:, :]))
                        nc.vector.tensor_tensor(ind[:, :], count, stage2[:, :], ALU.mult)
                        nc.vector.tensor_tensor(stage[:, :], total, stage2[:, :], ALU.mult).then_inc(s_mean, 1)
                        dve.wait_ge(s_rows_ps, n)
                        nc.vector.tensor_copy(rows_out[:, :, :], psB[:, :].rearrange("p (s f) -> p s f", s=TILES)).then_inc(s_rows_sb, 1)
                        nc.vector.tensor_copy(acc[:, :, bass.ds(c * CHUNK, CHUNK)], zero_col[:, :].unsqueeze(1).to_broadcast([P, 2, CHUNK]))
                        hold(dve, s_rows_st, n * 16)

                @block.tensor
                def _(pe):
                    hold(pe, s_nw, (layer + 1) * 96)
                    with pe.Fori(0, CHUNKS) as c:
                        n = layer * CHUNKS + c + 1
                        pe.wait_ge(s_mean, n)
                        nc.tensor.matmul(psA[:, :], w2[:, :], stage[:, :], start=True, stop=False)
                        nc.tensor.matmul(psA[:, :], b2_row[:, :], ind[0:1, :], start=False, stop=False)
                        nc.tensor.matmul(psA[:, :], wself[:, :], nodeT[:, bass.ds(c * CHUNK, CHUNK)], start=False, stop=True).then_inc(s_x_ps, 1)
                        pe.wait_ge(s_x_sb, n)
                        for s in range(TILES):
                            nc.tensor.matmul(psB[:, s * D:(s + 1) * D], x_stage[:, s * P:(s + 1) * P], w1x[:, :], start=True, stop=False)
                            last = nc.tensor.matmul(psB[:, s * D:(s + 1) * D], ones[0:1, :], b1_row[:, :], start=False, stop=True)
                        last.then_inc(s_rows_ps, 1)

                @block.scalar
                def _(act):
                    hold(act, s_nw, (layer + 1) * 96)
                    with act.Fori(0, CHUNKS) as c:
                        hold(act, s_x_ps, layer * CHUNKS + c + 1)
                        nc.scalar.activation(nodeT[:, bass.ds(c * CHUNK, CHUNK)], psA[:, :], ACT.Identity, bias=bself_col[:, :])
                        nc.scalar.activation(x_stage[:, :], psA[:, :], ACT.Identity, bias=bself_col[:, :]).then_inc(s_x_sb, 1)

        def layernorm(dve, chain, n, y, result, signal):
            chain.link(nc.vector.bn_stats(stats[:, :], y), held=True)
            nc.vector.bn_aggr(mv[:, :], stats[:, :]).then_inc(s_var, 1)
            dve.wait_ge(s_std, n)
            chain.link(nc.vector.reciprocal(rstd[:, :], std[:, :]))
            nc.vector.tensor_scalar(result, y, mv[:, 0:1], rstd[:, :], ALU.subtract, ALU.mult).then_inc(signal, 1)

        def root(act, n):
            act.wait_ge(s_var, n)
            nc.scalar.activation(std[:, :], mv[:, 1:2], ACT.Sqrt, bias=eps_col[:, :]).then_inc(s_std, 1)

        with nc.Block() as block:
            @block.sync
            def _(sp):
                def tile(t, rows):
                    sp.dma_start(rows_in[0:rows, 0, :], x[bass.ds(t * P, rows), :]).then_inc(s_x_in, 16)
                    sp.wait_ge(s_z, t + 1)
                    sp.dma_start(z_rows[bass.ds(t * P, P), :], z_out[:, :]).then_inc(s_z_st, 16)
                    sp.wait_ge(s_kv_sb, t + 1)
                    sp.dma_start(kv_rows[bass.ds(t * P, P), :], rows_out[:, 0:2, :].rearrange("p a f -> p (a f)")).then_inc(s_kv_st, 16)
                with sp.Fori(0, NTILES - 1) as t:
                    tile(t, P)
                tile(NTILES - 1, LAST_ROWS)
                sp.wait_ge(s_z_st, NTILES * 16)
                sp.wait_ge(s_kv_st, NTILES * 16)

            @block.scalar
            def _(act):
                nc.scalar.mul(tau_bq[:, :], bq_col[:, :], TAU).then_inc(s_tau_bq, 1)
                act.wait_ge(s_tau_bq, 1)
                with act.Fori(0, NTILES) as t:
                    nc.scalar.activation(x_stage[:, 0:P], nodeT[:, bass.ds(t * P, P)], ACT.Copy).then_inc(s_xs, 1)
                    root(act, t + 1)
                    act.wait_ge(s_zT_ps, t + 1)
                    nc.scalar.activation(zT[:, :], psC[:, 0:P], ACT.Copy).then_inc(s_zT, 1)
                    hold(act, s_q_ps, t + 1)
                    nc.scalar.activation(nodeT[:, bass.ds(t * P, P)], psD[:, 0:P], ACT.Identity, bias=tau_bq[:, :], scale=TAU)

            @block.tensor
            def _(pe):
                with pe.Fori(0, NTILES) as t:
                    pe.wait_ge(s_xs, t + 1)
                    nc.tensor.transpose(psA[:, 0:P], x_stage[:, 0:P], ident[:, :]).then_inc(s_x3, 1)
                    pe.wait_ge(s_z, t + 1)
                    nc.tensor.transpose(psC[:, 0:P], z_out[:, :], ident[:, :]).then_inc(s_zT_ps, 1)
                    pe.wait_ge(s_zT, t + 1)
                    nc.tensor.matmul(psD[:, 0:P], wq[:, :], zT[:, :], start=True, stop=True).then_inc(s_q_ps, 1)
                    nc.tensor.matmul(psB[:, 0:2 * D], zT[:, :], wkv[:, :], start=True, stop=False)
                    nc.tensor.matmul(psB[:, 0:2 * D], ones[0:1, :], bkv_row[:, :], start=False, stop=True).then_inc(s_kv_ps, 1)

            @block.vector
            def _(dve):
                nc.vector.memset(maxB[:, :], NO_MAX)
                with dve.Fori(0, NTILES) as t:
                    dve.wait_ge(s_x_in, (t + 1) * 16)
                    dve.wait_ge(s_x3, t + 1)
                    chain = Chain(dve, s_z_chain, t * 3)
                    chain.link(nc.vector.tensor_tensor(rows_out[:, 3, :], psA[:, 0:P], rows_in[:, 0, :], ALU.add))
                    layernorm(dve, chain, t + 1, rows_out[:, 3, :], z_out[:, :], s_z)
                    dve.wait_ge(s_kv_ps, t + 1)
                    nc.vector.tensor_copy(rows_out[:, 0:2, :].rearrange("p a f -> p (a f)"), psB[:, 0:2 * D]).then_inc(s_kv_sb, 1)
                    dve.wait_ge(s_kv_st, (t + 1) * 16)
                    hold(dve, s_z_st, (t + 1) * 16)

        with nc.Block() as block:
            @block.gpsimd
            def _(pool):
                with pool.Fori(0, ITERS) as it:
                    for u in range(SLOTS):
                        hold(pool, s_idx, N_LAYERS * GROUPS + it * SLOTS + u + 1)
                        for j in range(TILES):
                            nc.gpsimd.indirect_dma_start(kv[:, u, j, :], None, kv_rows[0:N_NODES, :],
                                                         bass.IndirectOffsetOnAxis(ap=idx[u][:, j:j + 1], axis=0)).then_inc(s_gather[u], 16)

            @block.scalar
            def _(act):
                def copy_idx(g, u):
                    hold(act, s_slot_free, N_LAYERS * GROUPS + g + 1)
                    nc.scalar.activation(idx[u][:, :], srcT[:, bass.ds(g, 1), :].rearrange("p a j -> p (a j)"), ACT.Copy).then_inc(s_idx, 1)
                def group(g, u):
                    act.wait_ge(s_keysT_ps, g + 1)
                    nc.scalar.activation(keysT[:, 0, :], psA[:, :], ACT.Copy).then_inc(s_keysT, 1)
                    act.wait_ge(s_shifted, g + 1)
                    nc.scalar.activation(decay[:, :], decay[:, :], ACT.Exp)
                    nc.scalar.activation(score[:, 0, :, :], score[:, 0, :, :], ACT.Exp).then_inc(s_probs, 1)
                for u in range(SLOTS):
                    copy_idx(u, u)
                with act.Fori(0, ITERS - 1) as it:
                    for u in range(SLOTS):
                        group(it * SLOTS + u, u)
                        copy_idx(it * SLOTS + u + SLOTS, u)
                for u in range(SLOTS):
                    group(GROUPS - SLOTS + u, u)

            @block.tensor
            def _(pe):
                regs = [nc.tensor.alloc_register(f"pbase{u}") for u in range(SLOTS)]
                with pe.Fori(0, ITERS) as it:
                    nc.tensor.load(regs, base_row[0:1, bass.ds(it * SLOTS, SLOTS)])
                    bases = [nc.tensor.snap(r, min_val=0, max_val=PAD_DST) for r in regs]
                    for u in range(SLOTS):
                        n = it * SLOTS + u + 1
                        hold(pe, s_gather[u], (N_LAYERS * ITERS + it + 1) * 64)
                        for j in range(TILES):
                            last = nc.tensor.transpose(psA[:, j * P:(j + 1) * P], kv[:, u, j, 0:D], ident[:, :])
                        last.then_inc(s_keysT_ps, 1)
                        hold(pe, s_keysT, n)
                        for j in range(TILES):
                            last = nc.tensor.matmul(psB[:, j * WIN:(j + 1) * WIN], keysT[:, 0, j * P:(j + 1) * P], nodeT[:, bass.ds(bases[u], WIN)], start=True, stop=True)
                        last.then_inc(s_score_ps, 1)
                        hold(pe, s_masked, n)
                        nc.tensor.transpose(psC[:, 0:P], score[:, 0, :, :].rearrange("p j w -> p (j w)"), ident[:, :]).then_inc(s_scoreT, 1)
                        hold(pe, s_diag, n)
                        nc.tensor.matmul(psD[:, 0:P], ones[:, :], diag[:, :], start=True, stop=True).then_inc(s_maxB_ps, 1)
                        hold(pe, s_probs, n)
                        for j in range(TILES):
                            nc.tensor.matmul(psE[:, 0:WIN], kv[:, u, j, D:2 * D], score[:, 0, j, :], start=(j == 0), stop=(j == TILES - 1))
                        nc.tensor.matmul(psF[:, 0:P], ones[:, :], score[:, 0, :, :].rearrange("p j w -> p (j w)"), start=True, stop=True).then_inc(s_mix, 1)

            @block.vector
            def _(dve):
                regs = [nc.vector.alloc_register(f"abase{u}") for u in range(SLOTS)]
                with dve.Fori(0, ITERS) as it:
                    nc.vector.load(regs, base_row[0:1, bass.ds(it * SLOTS, SLOTS)])
                    bases = [nc.vector.snap(r, min_val=0, max_val=PAD_DST) for r in regs]
                    for u in range(SLOTS):
                        n = it * SLOTS + u + 1
                        chain = Chain(dve, s_attn_chain, (n - 1) * 5)
                        chain.link(nc.vector.tensor_tensor(outside[:, :, :],
                                                iotaN[:, bass.ds(bases[u], WIN)].unsqueeze(1).to_broadcast([P, TILES, WIN]),
                                                dstT[:, bass.ds(it * SLOTS + u, 1), :].rearrange("p a j -> p j a").to_broadcast([P, TILES, WIN]),
                                                ALU.not_equal))
                        sc = score[:, 0, :, :].rearrange("p j w -> p (j w)")
                        dve.wait_ge(s_score_ps, n)
                        nc.vector.scalar_tensor_tensor(sc, outside[:, :, :].rearrange("p j w -> p (j w)"), MASKED, psB[:, 0:P], ALU.mult, ALU.add).then_inc(s_masked, 1)
                        dve.wait_ge(s_scoreT, n)
                        chain.link(nc.vector.reduce_max(gmax[:, :], psC[:, 0:P], AX.X))
                        nc.vector.tensor_scalar(diag[:, :], ident[:, :], gmax[:, :], None, ALU.mult).then_inc(s_diag, 1)
                        dve.wait_ge(s_maxB_ps, n)
                        win = maxB[:, bass.ds(bases[u], WIN)]
                        chain.link(nc.vector.reduce_max(group_max[:, :], psD[:, 0:P].rearrange("p (j w) -> p w j", j=TILES), AX.X))
                        chain.link(nc.vector.tensor_tensor(new_max[:, :], group_max[:, :], win, ALU.max))
                        nc.vector.tensor_tensor(decay[:, :], win, new_max[:, :], ALU.subtract)
                        nc.vector.tensor_tensor(score[:, 0, :, :], score[:, 0, :, :], new_max[:, :].unsqueeze(1).to_broadcast([P, TILES, WIN]), ALU.subtract).then_inc(s_shifted, 1)
                        dve.wait_ge(s_mix, n)
                        a = acc[:, :, bass.ds(bases[u], WIN)]
                        nc.vector.tensor_tensor(a, a, decay[:, :].unsqueeze(1).to_broadcast([P, 2, WIN]), ALU.mult)
                        nc.vector.tensor_copy(win, new_max[:, :])
                        chain.link(nc.vector.tensor_reduce(group_den[:, :], psF[:, 0:P].rearrange("p (j w) -> p w j", j=TILES), AX.X, ALU.add))
                        a0, a1 = acc[:, 0, bass.ds(bases[u], WIN)], acc[:, 1, bass.ds(bases[u], WIN)]
                        nc.vector.tensor_tensor(a1, a1, group_den[:, :], ALU.add)
                        nc.vector.tensor_tensor(a0, a0, psE[:, 0:WIN], ALU.add).then_inc(s_slot_free, 1)

        with nc.If(far > 0):
            with nc.Block() as block:
                @block.sync
                def _(sp):
                    sp.wait_ge(h_mix, GROUPS * TILES * CHUNKS + 1)

                @block.gpsimd
                def _(pool):
                    with pool.Fori(0, GROUPS) as g:
                        hold(pool, h_idx, g + 1)
                        for j in range(TILES):
                            nc.gpsimd.indirect_dma_start(kv[:, 0, j, :], None, kv_rows[0:N_NODES, :],
                                                         bass.IndirectOffsetOnAxis(ap=idx[0][:, j:j + 1], axis=0)).then_inc(h_gather, 16)

                @block.scalar
                def _(act):
                    with act.Fori(0, GROUPS) as g:
                        hold(act, h_mix, g * TILES * CHUNKS + 1)
                        nc.scalar.activation(idx[0][:, :], srcT[:, bass.ds(g, 1), :].rearrange("p a j -> p (a j)"), ACT.Copy).then_inc(h_idx, 1)
                        act.wait_ge(h_keysT_ps, g + 1)
                        nc.scalar.activation(keysT[:, 0, :], psA[:, :], ACT.Copy).then_inc(h_keysT, 1)
                        for j in range(TILES):
                            with act.Fori(0, CHUNKS) as c:
                                act.wait_ge(h_shifted, (g * TILES + j) * CHUNKS + c + 1)
                                nc.scalar.activation(wide[:, 2, :], wide[:, 2, :], ACT.Exp)
                                nc.scalar.activation(wide[:, 0, :], wide[:, 0, :], ACT.Exp).then_inc(h_probs, 1)

                @block.tensor
                def _(pe):
                    with pe.Fori(0, GROUPS) as g:
                        hold(pe, h_gather, (g + 1) * 64)
                        for j in range(TILES):
                            last = nc.tensor.transpose(psA[:, j * P:(j + 1) * P], kv[:, 0, j, 0:D], ident[:, :])
                        last.then_inc(h_keysT_ps, 1)
                        hold(pe, h_keysT, g + 1)
                        for j in range(TILES):
                            with pe.Fori(0, CHUNKS) as c:
                                m = (g * TILES + j) * CHUNKS + c + 1
                                nc.tensor.matmul(psB[:, :], keysT[:, 0, j * P:(j + 1) * P], nodeT[:, bass.ds(c * CHUNK, CHUNK)], start=True, stop=True).then_inc(h_score, 1)
                                hold(pe, h_masked, m)
                                for b in range(TILES):
                                    last = nc.tensor.transpose(psC[:, b * P:(b + 1) * P], wide[:, 0, b * P:(b + 1) * P], ident[:, :])
                                last.then_inc(h_scoreT, 1)
                                hold(pe, h_diag, m)
                                nc.tensor.matmul(psD[:, :], ones[:, :], stage[:, :], start=True, stop=True).then_inc(h_max, 1)
                                hold(pe, h_probs, m)
                                nc.tensor.matmul(psE[:, :], kv[:, 0, j, D:2 * D], wide[:, 0, :], start=True, stop=True)
                                nc.tensor.matmul(psF[:, :], ones[:, :], wide[:, 0, :], start=True, stop=True).then_inc(h_mix, 1)

                @block.vector
                def _(dve):
                    with dve.Fori(0, GROUPS) as g:
                        for j in range(TILES):
                            with dve.Fori(0, CHUNKS) as c:
                                m = (g * TILES + j) * CHUNKS + c + 1
                                chain = Chain(dve, h_chain, (m - 1) * 4)
                                chain.link(nc.vector.tensor_tensor(wide[:, 1, :], iotaN[:, bass.ds(c * CHUNK, CHUNK)],
                                                                   far_dst[:, bass.ds(g, 1), j].to_broadcast([P, CHUNK]), ALU.not_equal))
                                dve.wait_ge(h_score, m)
                                nc.vector.scalar_tensor_tensor(wide[:, 0, :], wide[:, 1, :], MASKED, psB[:, :], ALU.mult, ALU.add).then_inc(h_masked, 1)
                                dve.wait_ge(h_scoreT, m)
                                chain.link(nc.vector.reduce_max(gmax4[:, :], psC[:, :].rearrange("p (b e) -> p b e", b=TILES), AX.X))
                                nc.vector.tensor_tensor(stage[:, :].rearrange("p (b w) -> p b w", b=TILES), ident[:, :].unsqueeze(1).to_broadcast([P, TILES, P]),
                                                        gmax4[:, :].unsqueeze(2).to_broadcast([P, TILES, P]), ALU.mult).then_inc(h_diag, 1)
                                dve.wait_ge(h_max, m)
                                win = maxB[:, bass.ds(c * CHUNK, CHUNK)]
                                chain.link(nc.vector.tensor_tensor(wide[:, 3, :], psD[:, :], win, ALU.max))
                                nc.vector.tensor_tensor(wide[:, 2, :], win, wide[:, 3, :], ALU.subtract)
                                nc.vector.tensor_tensor(wide[:, 0, :], wide[:, 0, :], wide[:, 3, :], ALU.subtract).then_inc(h_shifted, 1)
                                dve.wait_ge(h_mix, m + 1)
                                a = acc[:, :, bass.ds(c * CHUNK, CHUNK)]
                                nc.vector.tensor_tensor(a, a, wide[:, 2, :].unsqueeze(1).to_broadcast([P, 2, CHUNK]), ALU.mult)
                                chain.link(nc.vector.tensor_copy(win, wide[:, 3, :]))
                                a0, a1 = acc[:, 0, bass.ds(c * CHUNK, CHUNK)], acc[:, 1, bass.ds(c * CHUNK, CHUNK)]
                                nc.vector.tensor_tensor(a0, a0, psE[:, :], ALU.add)
                                nc.vector.tensor_tensor(a1, a1, psF[:, :], ALU.add)

        with nc.Block() as block:
            @block.sync
            def _(sp):
                def tile(t, rows):
                    sp.dma_start(rows_in[:, 0, :], z_rows[bass.ds(t * P, P), :]).then_inc(s_z_in, 16)
                    sp.wait_ge(s_o, t + 1)
                    sp.dma_start(out[bass.ds(t * P, rows), :], z_out[0:rows, :]).then_inc(s_out, 16)
                with sp.Fori(0, NTILES - 1) as t:
                    tile(t, P)
                tile(NTILES - 1, LAST_ROWS)
                sp.wait_ge(s_out, NTILES * 16)

            @block.scalar
            def _(act):
                with act.Fori(0, NTILES) as t:
                    root(act, t + 1 + NTILES)

            @block.tensor
            def _(pe):
                with pe.Fori(0, NTILES) as t:
                    pe.wait_ge(s_h, t + 1)
                    nc.tensor.transpose(psA[:, 0:P], stage[:, 0:P], ident[:, :]).then_inc(s_hT, 1)

            @block.vector
            def _(dve):
                with dve.Fori(0, NTILES) as t:
                    den = acc[:, 1, bass.ds(t * P, P)]
                    chain = Chain(dve, s_out_chain, t * 5)
                    chain.link(nc.vector.scalar_tensor_tensor(stage2[:, 0:P], den, 0.0, den, ALU.is_equal, ALU.add))
                    chain.link(nc.vector.reciprocal(stage2[:, 0:P], stage2[:, 0:P]))
                    nc.vector.tensor_tensor(stage[:, 0:P], acc[:, 0, bass.ds(t * P, P)], stage2[:, 0:P], ALU.mult).then_inc(s_h, 1)
                    dve.wait_ge(s_z_in, (t + 1) * 16)
                    dve.wait_ge(s_hT, t + 1)
                    chain.link(nc.vector.tensor_tensor(rows_out[:, 3, :], psA[:, 0:P], rows_in[:, 0, :], ALU.add))
                    layernorm(dve, chain, t + 1 + NTILES, rows_out[:, 3, :], z_out[:, :], s_o)
                    hold(dve, s_out, (t + 1) * 16)



def kernel(**inputs):
    import numpy as _np
    import concourse.bacc as _bacc
    from concourse import mybir as _mybir
    from concourse.bass_utils import run_bass_kernel_spmd as _run
    nc = _bacc.Bacc("TRN2", target_bir_lowering=False, num_devices=1)
    names = ["x", "src", "dst", "edge_attr_16", "L0_gnn_W1", "L0_gnn_b1", "L0_gnn_W2", "L0_gnn_b2", "L0_gnn_Wself", "L0_gnn_bself",
             "L1_gnn_Wq", "L1_gnn_bq", "L1_gnn_Wk", "L1_gnn_bk", "L1_gnn_Wv", "L1_gnn_bv"]
    arrays, args = {}, []
    for name in names:
        a = _np.ascontiguousarray(inputs[name])
        arrays[f"in_{name}"] = a
        args.append(nc.dram_tensor(f"in_{name}", a.shape, _mybir.dt.from_np(a.dtype), kind="ExternalInput").ap())
    out = nc.dram_tensor("out", (N_NODES, D), _mybir.dt.float32, kind="ExternalOutput").ap()
    gnn_attention(nc, *args, out)
    r = _run(nc, [arrays], core_ids=[0])
    return r.results[0]["out"]
```

```python
from contextlib import ExitStack

import concourse.bass as bass
from concourse import mybir

P = 128
N_NODES, N_EDGES, D, DE, N_LAYERS = 6250, 200000, 128, 16, 3
TILES = 4
GROUP = P * TILES
SLOTS = 8
ROWS = 98
ROUNDS = 4
GROUPS = ROWS * ROUNDS
WIN = 32
CHUNK = 512
CHUNKS = 13
NODES = CHUNK * CHUNKS
NTILES = -(-N_NODES // P)
LAST_ROWS = N_NODES - (NTILES - 1) * P
KV = D + 3 * D // 2
PAD_DST = N_NODES
EPS = 1e-5
TAU = float(D) ** -0.5
MASKED = -1e30
NO_MAX = -1e20

fp32 = mybir.dt.float32
bf16 = mybir.dt.bfloat16
i32 = mybir.dt.int32
ALU = mybir.AluOpType
ACT = mybir.ActivationFunctionType
AX = mybir.AxisListType


def gnn_attention(nc, x, src, dst, edge_attr, W1, b1, W2, b2, Wself, bself, Wq, bq, Wk, bk, Wv, bv, out):
    ctx = ExitStack()
    with ctx:
        def sb(name, shape, dt=fp32):
            return ctx.enter_context(nc.sbuf_tensor(name, shape, dt))

        def ps(name, shape, dt=fp32):
            return ctx.enter_context(nc.psum_tensor(name, shape, dt))

        def sem(name):
            return ctx.enter_context(nc.semaphore(name))

        gather_rows = nc.dram_tensor("gather_rows", (NODES, D), fp32, kind="Internal").ap()
        kv_rows = nc.dram_tensor("kv_rows", (NODES, KV), fp32, kind="Internal").ap()
        z_rows = nc.dram_tensor("z_rows", (NODES, D), fp32, kind="Internal").ap()
        base_dram = nc.dram_tensor("base_dram", (ROUNDS, ROWS), i32, kind="Internal").ap()

        nodeT = sb("nodeT", [P, NODES])
        acc = sb("acc", [P, 2, NODES])
        maxB = sb("maxB", [P, NODES])
        iota = sb("iota", [P, CHUNK])
        chunk_start = sb("chunk_start", [P, CHUNKS])
        dstT = sb("dstT", [P, GROUPS, TILES])
        srcT = sb("srcT", [P, GROUPS, TILES], i32)
        base_row = sb("base_row", [1, GROUPS + 2], i32)
        ident = sb("ident", [P, P])
        ones = sb("ones", [P, P])
        ones_h = sb("ones_h", [P, P], bf16)
        w1x = sb("w1x", [P, D])
        w1e = sb("w1e", [TILES * DE, TILES, D])
        w2 = sb("w2", [P, D])
        wself = sb("wself", [P, D])
        b1_row = sb("b1_row", [1, D])
        b2_row = sb("b2_row", [1, D])
        bself_col = sb("bself_col", [P, 1])
        wq = sb("wq", [P, D])
        wkv = sb("wkv", [P, 2 * D])
        bkv_row = sb("bkv_row", [1, 2 * D])
        bq_col = sb("bq_col", [P, 1])
        idx = [sb(f"idx{s}", [P, TILES], i32) for s in range(SLOTS)]
        attr = sb("attr", [P, SLOTS, TILES * DE])
        attrT = sb("attrT", [TILES * DE, SLOTS, P])
        onehot = sb("onehot", [P, 2, TILES, WIN], bf16)
        work = sb("work", [P, SLOTS * TILES * KV])
        msg = work[:, 0:SLOTS * TILES * D].rearrange("p (s j f) -> p s j f", s=SLOTS, j=TILES)
        kv = work[:, :].rearrange("p (s j f) -> p s j f", s=SLOTS, j=TILES)
        kv_out = sb("kv_out", [P, KV])
        natural = work[0:ROWS, 0:ROUNDS * GROUP].rearrange("p (r e) -> p r e", r=ROUNDS)
        natural_i = work[0:ROWS, ROUNDS * GROUP:2 * ROUNDS * GROUP].bitcast(i32).rearrange("p (r e) -> p r e", r=ROUNDS)
        shared = sb("shared", [P, 2 * 3 * TILES * D // 2])
        parts = shared[:, :].bitcast(bf16).rearrange("p (b k j f) -> p b k j f", b=2, k=3, j=TILES)
        keysT = shared[:, 0:TILES * P]
        tiles = 2 * TILES * WIN
        score = shared[:, TILES * P:TILES * P + tiles].rearrange("p (b j w) -> p b j w", b=2, j=TILES)
        outside = shared[:, TILES * P + tiles:TILES * P + 2 * tiles].rearrange("p (b j w) -> p b j w", b=2, j=TILES)
        probs = shared[:, TILES * P + 2 * tiles:TILES * P + 2 * tiles + 3 * tiles // 2].bitcast(bf16).rearrange("p (b k j w) -> p b k j w", b=2, k=3, j=TILES)
        diag = sb("diag", [P, P])
        gmax = sb("gmax", [P, 1])
        gmax4 = sb("gmax4", [P, TILES])
        group_max = sb("group_max", [P, WIN])
        new_max = sb("new_max", [P, WIN])
        decay = sb("decay", [P, 2, WIN])
        rows_in = sb("rows_in", [P, 2, D])
        stage = sb("stage", [P, CHUNK])
        stage2 = sb("stage2", [P, CHUNK])
        ind = sb("ind", [P, CHUNK])
        x_stage = sb("x_stage", [P, CHUNK])
        group_den = sb("group_den", [P, WIN])
        tau_bq = sb("tau_bq", [P, 1])
        rows_out = sb("rows_out", [P, TILES, D])
        z_out = sb("z_out", [P, D])
        zT = sb("zT", [P, P])
        stats = sb("stats", [P, 6])
        mv = sb("mv", [P, 2])
        std = sb("std", [P, 1])
        rstd = sb("rstd", [P, 1])
        base_i = sb("base_i", [ROWS, ROUNDS], i32)
        eps_col = sb("eps_col", [P, 1])
        far_dst = sb("far_dst", [P, GROUPS, TILES])
        far_i = sb("far_i", [1, 1], i32)
        rel = sb("rel", [P, TILES])
        is_far = work[:, 0:GROUPS * TILES].rearrange("p (g j) -> p g j", g=GROUPS)
        base_all = work[:, GROUPS * TILES:GROUPS * TILES + GROUPS]
        base_all_i = work[:, GROUPS * TILES + GROUPS:GROUPS * TILES + 2 * GROUPS].bitcast(i32)
        wide = work[:, TILES * CHUNK:2 * TILES * CHUNK].rearrange("p (j w) -> p j w", j=TILES)
        zero_col = sb("zero_col", [P, 1])

        psA = ps("psA", [P, 512])
        psB = ps("psB", [P, 512])
        psC = ps("psC", [P, 512])
        psD = ps("psD", [P, 512])
        psE = ps("psE", [P, 512])
        psF = ps("psF", [P, 512])
        psG = ps("psG", [P, 512])
        psH = ps("psH", [P, 512])

        s_w = sem("s_w")
        s_layer_w = sem("s_layer_w")
        s_const = sem("s_const")
        s_attr = [sem(f"s_attr{s}") for s in range(SLOTS)]
        s_gather = [sem(f"s_gather{s}") for s in range(SLOTS)]
        s_idx = sem("s_idx")
        s_pool = sem("s_pool")
        s_slot_free = sem("s_slot_free")
        s_attrT = sem("s_attrT")
        s_attrT_sb = sem("s_attrT_sb")
        s_edge_term = sem("s_edge_term")
        s_pre = sem("s_pre")
        s_part0 = sem("s_part0")
        s_rest = sem("s_rest")
        s_part1 = sem("s_part1")
        s_parts = sem("s_parts")
        s_onehot = sem("s_onehot")
        s_scatter = sem("s_scatter")
        s_node = {}

        def seq(name):
            if name not in s_node:
                s_node[name] = sem("prep_" + name)
            return s_node[name]

        s_diag = sem("s_diag")
        s_h = sem("s_h")
        s_hT = sem("s_hT")
        s_keysT = sem("s_keysT")
        s_keysT_ps = sem("s_keysT_ps")
        s_kv_ps = sem("s_kv_ps")
        s_kv_sb = sem("s_kv_sb")
        s_kv_st = sem("s_kv_st")
        s_masked = sem("s_masked")
        s_maxB_ps = sem("s_maxB_ps")
        s_mean = sem("s_mean")
        s_mix = sem("s_mix")
        s_nw = sem("s_nw")
        s_o = sem("s_o")
        s_out = sem("s_out")
        s_probs = sem("s_probs")
        s_q_ps = sem("s_q_ps")
        s_rows_ps = sem("s_rows_ps")
        s_rows_sb = sem("s_rows_sb")
        s_rows_st = sem("s_rows_st")
        s_scoreT = sem("s_scoreT")
        s_score_ps = sem("s_score_ps")
        s_shifted = sem("s_shifted")
        s_std = sem("s_std")
        s_var = sem("s_var")
        s_x3 = sem("s_x3")
        s_x_in = sem("s_x_in")
        s_x_ps = sem("s_x_ps")
        s_x_sb = sem("s_x_sb")
        s_xs = sem("s_xs")
        s_z = sem("s_z")
        s_zT = sem("s_zT")
        s_zT_ps = sem("s_zT_ps")
        s_z_in = sem("s_z_in")
        s_z_st = sem("s_z_st")
        s_tau_bq = sem("s_tau_bq")
        s_den_chain = sem("s_den_chain")
        s_outside, s_gmax, s_prob0, s_prob_rest, s_prob1, s_terms = [sem(n) for n in ("s_outside", "s_gmax", "s_prob0", "s_prob_rest", "s_prob1", "s_terms")]
        f_attr = sem("f_attr")
        f_rel = sem("f_rel")
        f_attrT = sem("f_attrT")
        f_attrT_sb = sem("f_attrT_sb")
        f_gather = sem("f_gather")
        f_idx = sem("f_idx")
        f_onehot = sem("f_onehot")
        f_pre = sem("f_pre")
        f_relu = sem("f_relu")
        f_scatter = sem("f_scatter")
        f_term = sem("f_term")
        h_chain = sem("h_chain")
        h_diag = sem("h_diag")
        h_gather = sem("h_gather")
        h_idx = sem("h_idx")
        h_keysT = sem("h_keysT")
        h_keysT_ps = sem("h_keysT_ps")
        h_masked = sem("h_masked")
        h_max = sem("h_max")
        h_mix = sem("h_mix")
        h_probs = sem("h_probs")
        h_score = sem("h_score")
        h_value = sem("h_value")
        h_scoreT = sem("h_scoreT")
        h_shifted = sem("h_shifted")
        s_tick = sem("s_tick")

        def hold(engine, semaphore, value):
            engine.wait_ge(semaphore, value)
            engine.sem_inc(s_tick, 1)

        class Chain:
            def __init__(self, engine, semaphore, before):
                self.engine, self.semaphore, self.count = engine, semaphore, before

            def link(self, instruction, held=False):
                instruction.then_inc(self.semaphore, 1)
                self.count = self.count + 1
                self.engine.wait_ge(self.semaphore, self.count)
                if held:
                    self.engine.sem_inc(s_tick, 1)

        s_node_chain, s_z_chain, s_attn_chain, s_out_chain = sem("s_node_chain"), sem("s_z_chain"), sem("s_attn_chain"), sem("s_out_chain")

        s_load, s_ld2 = sem("s_load"), sem("s_ld2")
        s_nat, s_tp, s_tc = sem("s_nat"), sem("s_tp"), sem("s_tc")
        s_v = sem("s_v")
        psX = [psA, psB]
        FULL = N_EDGES // GROUP - 3 * ROWS
        REST = N_EDGES % GROUP
        with nc.Block() as block:
            @block.sync
            def _(sp):
                for n, table in enumerate((dst, src)):
                    if n:
                        sp.wait_ge(s_nat, 5)
                    else:
                        sp.wait_ge(s_nat, 1)
                    for r in range(ROUNDS - 1):
                        sp.dma_start(natural_i[:, r, :], table[r * ROWS * GROUP:(r + 1) * ROWS * GROUP]
                                     .rearrange("(p e) -> p e", e=GROUP)).then_inc(s_load, 16)
                    o = (ROUNDS - 1) * ROWS * GROUP
                    sp.dma_start(natural_i[0:FULL, 3, :], table[o:o + FULL * GROUP].rearrange("(p e) -> p e", e=GROUP)).then_inc(s_load, 16)
                    sp.dma_start(natural_i[FULL:FULL + 1, 3, 0:REST], table[o + FULL * GROUP:N_EDGES].rearrange("(p e) -> p e", p=1)).then_inc(s_load, 16)
                sp.wait_ge(s_nat, 3)
                with nc.allow_non_contiguous_dma(reason="392 numbers, once"):
                    sp.dma_start(base_dram.rearrange("r p -> p r"), base_i[:, :]).then_inc(s_ld2, 16)
                sp.wait_ge(s_ld2, 16)
                sp.dma_start(base_row[:, 0:GROUPS], base_dram.rearrange("(a r) p -> a (r p)", a=1)).then_inc(s_ld2, 16)
                sp.wait_ge(s_ld2, 32)

            @block.scalar
            def _(act):
                act.dma_start(wq[:, :], Wq).then_inc(s_w, 16)
                act.dma_start(wkv[:, 0:D], Wk).then_inc(s_w, 16)
                act.dma_start(wkv[:, D:2 * D], Wv).then_inc(s_w, 16)
                act.dma_start(bkv_row[:, 0:D], bk.rearrange("(a f) -> a f", a=1)).then_inc(s_w, 16)
                act.dma_start(bkv_row[:, D:2 * D], bv.rearrange("(a f) -> a f", a=1)).then_inc(s_w, 16)
                act.dma_start(bq_col[:, :], bq.rearrange("(p a) -> p a", a=1)).then_inc(s_w, 16)
                act.wait_ge(s_w, 96)

            @block.gpsimd
            def _(pool):
                pool.memset(ident[:, :], 0.0).then_inc(s_const, 1)
                pool.memset(ones[:, :], 1.0)
                pool.memset(ones_h[:, :], 1.0)
                pool.wait_ge(s_const, 1)
                pool.affine_select(out=ident[:, :], in_=ident[:, :], compare_op=ALU.not_equal, fill=1.0, base=0,
                                   pattern=[[-1, P]], channel_multiplier=1).then_inc(s_const, 1)
                pool.iota(iota[:, :], pattern=[[1, CHUNK]], base=0, channel_multiplier=0,
                          allow_small_or_imprecise_dtypes=True).then_inc(s_const, 1)
                pool.iota(chunk_start[:, :], pattern=[[CHUNK, CHUNKS]], base=0, channel_multiplier=0,
                          allow_small_or_imprecise_dtypes=True)
                pool.memset(w1e[:, :, :], 0.0)
                pool.memset(attr[:, :, :], 0.0).then_inc(s_const, 1)

            @block.vector
            def _(dve):
                dve.sem_inc(s_slot_free, SLOTS)
                dve.sem_inc(f_scatter, 1)
                dve.sem_inc(h_mix, 1)
                nc.vector.memset(base_row[:, GROUPS:GROUPS + 2], 0)
                nc.vector.memset(eps_col[:, :], EPS)
                nc.vector.memset(zero_col[:, :], 0.0)
                nc.vector.memset(nodeT[:, :], 0.0)
                nc.vector.memset(acc[:, :, :], 0.0)
                nc.vector.memset(natural_i[:, 3, :], PAD_DST).then_inc(s_nat, 1)
                dve.wait_ge(s_load, 80)
                nc.vector.tensor_copy(natural[:, :, :], natural_i[:, :, :]).then_inc(s_nat, 1)
                dve.wait_ge(s_nat, 2)
                nc.vector.tensor_reduce(base_i[:, :], natural[:, :, :], AX.X, ALU.min).then_inc(s_nat, 1)
                for n in range(2):
                    for t in range(16):
                        r, j = t // 4, t % 4
                        dve.wait_ge(s_tp, 16 * n + t + 1)
                        table = srcT if n else dstT
                        nc.vector.tensor_copy(table[:, r * ROWS:(r + 1) * ROWS, j], psX[t % 2][:, 0:ROWS]).then_inc(s_tc, 1)
                    if n == 0:
                        nc.vector.memset(natural_i[:, 3, :], 0).then_inc(s_nat, 1)
                        dve.wait_ge(s_nat, 4)
                        dve.wait_ge(s_tp, 16)
                        dve.sem_inc(s_nat, 1)
                        dve.wait_ge(s_load, 160)
                        nc.vector.tensor_copy(natural[:, :, :], natural_i[:, :, :]).then_inc(s_nat, 1)

            @block.tensor
            def _(pe):
                pe.wait_ge(s_const, 2)
                for n in range(2):
                    pe.wait_ge(s_nat, 6 if n else 2)
                    for t in range(16):
                        r, j = t // 4, t % 4
                        if 16 * n + t >= 2:
                            pe.wait_ge(s_tc, 16 * n + t - 1)
                        nc.tensor.transpose(psX[t % 2][:, 0:ROWS], natural[:, r, j:GROUP:TILES], ident[0:ROWS, 0:ROWS]).then_inc(s_tp, 1)

        s_base, s_far_chain, s_far = sem("s_base"), sem("s_far_chain"), sem("s_far")
        with nc.Block() as block:
            @block.sync
            def _(sp):
                sp.dma_start(base_all_i[:, :], base_dram.rearrange("(a r) p -> a (r p)", a=1).to_broadcast([P, GROUPS])).then_inc(s_base, 16)

            @block.vector
            def _(dve):
                chain = Chain(dve, s_far_chain, 0)
                dve.wait_ge(s_base, 16)
                chain.link(nc.vector.tensor_copy(base_all[:, :], base_all_i[:, :]))
                each_base = base_all[:, :].unsqueeze(2).to_broadcast([P, GROUPS, TILES])
                nc.vector.tensor_scalar(far_dst[:, :, :], dstT[:, :, :], 1.0, None, ALU.add)
                chain.link(nc.vector.tensor_tensor(is_far, dstT[:, :, :], each_base, ALU.subtract))
                chain.link(nc.vector.tensor_copy(dstT[:, :, :], is_far))
                chain.link(nc.vector.scalar_tensor_tensor(far_dst[:, :, :], dstT[:, :, :], float(WIN), far_dst[:, :, :], ALU.is_ge, ALU.mult))
                chain.link(nc.vector.tensor_scalar(far_dst[:, :, :], far_dst[:, :, :], -1.0, None, ALU.add))
                chain.link(nc.vector.tensor_reduce(gmax[:, :], far_dst[:, :, :].rearrange("p g j -> p (g j)"), AX.X, ALU.max))
                chain.link(nc.vector.tensor_scalar(diag[:, :], ident[:, :], gmax[:, :], None, ALU.mult))
                dve.wait_ge(s_far, 1)
                chain.link(nc.vector.tensor_reduce(gmax[0:1, :], psA[0:1, 0:P], AX.X, ALU.max))
                chain.link(nc.vector.tensor_scalar(gmax[0:1, :], gmax[0:1, :], 0.0, None, ALU.is_ge))
                chain.link(nc.vector.tensor_copy(far_i[:, :], gmax[0:1, :]))

            @block.tensor
            def _(pe):
                pe.wait_ge(s_far_chain, 7)
                nc.tensor.matmul(psA[:, 0:P], ones[:, :], diag[:, :], start=True, stop=True).then_inc(s_far, 1)

        far = nc.values_load(far_i[0:1, 0:1], min_val=0, max_val=1)

        s_wl = sem("s_wl")
        with nc.Block() as block:
            @block.sync
            def _(sp):
                sp.dma_start(w1x[:, :], W1[0, 0:D, :]).then_inc(s_wl, 16)
                sp.dma_start(b1_row[:, :], b1[0:1, :]).then_inc(s_wl, 16)
                s = seq("x_in")
                def load(t, rows):
                    sp.wait_ge(seq("xT_ps"), t)
                    sp.dma_start(rows_in[0:rows, 0, :], x[bass.ds(t * P, rows), :]).then_inc(s, 16)
                sp.dma_start(rows_in[:, 0, :], x[0:P, :]).then_inc(s, 16)
                with sp.Fori(1, NTILES - 1) as t:
                    load(t, P)
                load(NTILES - 1, LAST_ROWS)

            @block.tensor
            def _(pe):
                pe.wait_ge(s_wl, 32)
                def tile(t, rows):
                    pe.wait_ge(seq("x_in"), (t + 1) * 16)
                    nc.tensor.transpose(psA[:, 0:rows], rows_in[0:rows, 0, :], ident[0:rows, 0:rows]).then_inc(seq("xT_ps"), 1)
                    pe.wait_ge(s_v, t + 1)
                    nc.tensor.matmul(psB[0:rows, 0:D], stage[:, 0:rows], w1x[:, :], start=True, stop=False)
                    nc.tensor.matmul(psB[0:rows, 0:D], ones[0:1, 0:rows], b1_row[:, :], start=False, stop=True).then_inc(seq("row0_ps"), 1)
                with pe.Fori(0, NTILES - 1) as t:
                    tile(t, P)
                tile(NTILES - 1, LAST_ROWS)

            @block.vector
            def _(dve):
                def tile(t, rows):
                    dve.wait_ge(seq("xT_ps"), t + 1)
                    nc.vector.tensor_copy(stage[:, 0:rows], psA[:, 0:rows])
                    nc.vector.tensor_copy(nodeT[:, bass.ds(t * P, rows)], psA[:, 0:rows]).then_inc(s_v, 1)
                    dve.wait_ge(seq("row0_ps"), t + 1)
                    nc.vector.tensor_copy(rows_out[0:rows, 0, :], psB[0:rows, 0:D]).then_inc(seq("row0_sb"), 1)
                    dve.wait_ge(seq("row0_st"), (t + 1) * 16)
                with dve.Fori(0, NTILES - 1) as t:
                    tile(t, P)
                tile(NTILES - 1, LAST_ROWS)

            @block.scalar
            def _(act):
                def tile(t, rows):
                    act.wait_ge(seq("row0_sb"), t + 1)
                    act.dma_start(gather_rows[bass.ds(t * P, rows), :], rows_out[0:rows, 0, :]).then_inc(seq("row0_st"), 16)
                with act.Fori(0, NTILES - 1) as t:
                    tile(t, P)
                tile(NTILES - 1, LAST_ROWS)
                act.wait_ge(seq("row0_st"), NTILES * 16)

        ITERS = GROUPS // SLOTS
        with nc.Fori(0, N_LAYERS) as layer:
            with nc.Block() as block:
                @block.sync
                def _(sp):
                    for j in range(TILES):
                        sp.dma_start(w1e[DE * j:DE * (j + 1), j, :], W1[bass.ds(layer, 1), D:D + DE, :].rearrange("a k f -> (a k) f")).then_inc(s_layer_w, 16)
                    def load(g, u, start, edges=GROUP):
                        sp.wait_ge(s_slot_free, layer * GROUPS + g + 1)
                        sp.dma_start(attr[0:edges // TILES, u, :],
                                     edge_attr[bass.ds(start, edges), :].rearrange("(p j) k -> p (j k)", j=TILES)).then_inc(s_attr[u], 16)
                    with sp.Fori(0, ITERS - 1) as it:
                        for u in range(SLOTS):
                            load(it * SLOTS + u, u, (it * SLOTS + u) * GROUP)
                    for u in range(SLOTS - 2):
                        load(GROUPS - SLOTS + u, u, (GROUPS - SLOTS + u) * GROUP)
                    load(GROUPS - 2, SLOTS - 2, (GROUPS - 2) * GROUP, REST)
                    load(GROUPS - 1, SLOTS - 1, N_EDGES - GROUP)
                    hold(sp, s_layer_w, (layer + 1) * 64)

                @block.gpsimd
                def _(pool):
                    with pool.Fori(0, ITERS) as it:
                        for u in range(SLOTS):
                            hold(pool, s_idx, layer * GROUPS + it * SLOTS + u + 1)
                            for j in range(TILES):
                                nc.gpsimd.indirect_dma_start(msg[:, u, j, :], None, gather_rows[0:N_NODES, :],
                                                             bass.IndirectOffsetOnAxis(ap=idx[u][:, j:j + 1], axis=0)).then_inc(s_gather[u], 16)

                @block.scalar
                def _(act):
                    def copy_idx(g, u):
                        hold(act, s_slot_free, layer * GROUPS + g + 1)
                        nc.scalar.activation(idx[u][:, :], srcT[:, bass.ds(g, 1), :].rearrange("p a j -> p (a j)"), ACT.Copy).then_inc(s_idx, 1)

                    def attr_copy(g, u):
                        act.wait_ge(s_attrT, layer * GROUPS + g + 1)
                        nc.scalar.activation(attrT[:, u, :], (psC, psD)[u % 2][0:TILES * DE, 0:P], ACT.Copy).then_inc(s_attrT_sb, 1)

                    def split(g, u):
                        act.wait_ge(s_pre, layer * GROUPS + g + 1)
                        nc.scalar.activation(parts[:, u % 2, 0, :, :], msg[:, u, :, :], ACT.Relu).then_inc(s_part0, 1)
                        act.wait_ge(s_rest, layer * GROUPS + g + 1)
                        nc.scalar.activation(parts[:, u % 2, 1, :, :], msg[:, u, :, :], ACT.Copy).then_inc(s_part1, 1)

                    for u in range(SLOTS - 1):
                        copy_idx(u, u)
                    attr_copy(0, 0)
                    attr_copy(1, 1)
                    with act.Fori(0, ITERS - 1) as it:
                        for u in range(SLOTS):
                            g = it * SLOTS + u
                            split(g, u)
                            attr_copy(g + 2, (u + 2) % SLOTS)
                            copy_idx(g + SLOTS - 1, (u + SLOTS - 1) % SLOTS)
                    for u in range(SLOTS):
                        g = GROUPS - SLOTS + u
                        split(g, u)
                        if u + 2 < SLOTS:
                            attr_copy(g + 2, u + 2)
                        if u == 0:
                            copy_idx(g + SLOTS - 1, SLOTS - 1)

                @block.tensor
                def _(pe):
                    def attr_transpose(g, u, it):
                        hold(pe, s_attr[u], (layer * ITERS + it + 1) * 16)
                        nc.tensor.transpose((psC, psD)[u % 2][0:TILES * DE, 0:P], attr[:, u, :], ident[:, :]).then_inc(s_attrT, 1)

                    def edge_term(g, u):
                        pe.wait_ge(s_attrT_sb, layer * GROUPS + g + 1)
                        nc.tensor.matmul((psA, psB)[u % 2][:, :], attrT[:, u, :], w1e[:, :, :].rearrange("p j f -> p (j f)"),
                                         start=True, stop=True).then_inc(s_edge_term, 1)

                    def scatter(g, u):
                        n = layer * GROUPS + g + 1
                        total = (psE, psF)[u % 2]
                        pe.wait_ge(s_onehot, n)
                        for j in range(TILES):
                            nc.tensor.matmul(total[:, WIN:2 * WIN], ones_h[:, :], onehot[:, u % 2, j, :], start=(j == 0), stop=(j == TILES - 1))
                        pe.wait_ge(s_parts, n)
                        for k in range(3):
                            for j in range(TILES):
                                last = nc.tensor.matmul(total[:, 0:WIN], parts[:, u % 2, k, j, :], onehot[:, u % 2, j, :],
                                                        start=(k + j == 0), stop=(k == 2 and j == TILES - 1))
                        last.then_inc(s_scatter, 1)

                    hold(pe, s_layer_w, (layer + 1) * 64)
                    attr_transpose(0, 0, 0)
                    attr_transpose(1, 1, 0)
                    edge_term(0, 0)
                    with pe.Fori(0, ITERS - 1) as it:
                        for u in range(SLOTS):
                            g = it * SLOTS + u
                            edge_term(g + 1, (u + 1) % SLOTS)
                            attr_transpose(g + 2, (u + 2) % SLOTS, it + (u + 2) // SLOTS)
                            scatter(g, u)
                    for u in range(SLOTS):
                        g = GROUPS - SLOTS + u
                        if u + 1 < SLOTS:
                            edge_term(g + 1, u + 1)
                        if u + 2 < SLOTS:
                            attr_transpose(g + 2, u + 2, ITERS - 1)
                        scatter(g, u)

                @block.vector
                def _(dve):
                    regs = [nc.vector.alloc_register(f"base{u}") for u in range(SLOTS + 1)]

                    def load_bases(first, count):
                        nc.vector.load(regs[0:count], base_row[0:1, bass.ds(first, count)])
                        return [nc.vector.snap(r, min_val=0, max_val=PAD_DST) for r in regs[0:count]]

                    def third_part(g, u):
                        dve.wait_ge(s_part1, layer * GROUPS + g + 1)
                        nc.vector.tensor_tensor(parts[:, u % 2, 2, :, :], msg[:, u, :, :], parts[:, u % 2, 1, :, :], ALU.subtract).then_inc(s_parts, 1)

                    def accumulate(g, u, base):
                        dve.wait_ge(s_scatter, layer * GROUPS + g + 1)
                        a = acc[:, :, bass.ds(base, WIN)]
                        nc.vector.tensor_tensor(a, a, (psE, psF)[u % 2][:, 0:2 * WIN].rearrange("p (c w) -> p c w", c=2), ALU.add).then_inc(s_slot_free, 1)

                    def step(it, u, base, base_before, first=False):
                        g = it * SLOTS + u
                        before = (u - 1) % SLOTS
                        m = msg[:, u, :, :].rearrange("p j f -> p (j f)")
                        dve.wait_ge(s_gather[u], (layer * ITERS + it + 1) * 64)
                        dve.wait_ge(s_edge_term, layer * GROUPS + g + 1)
                        nc.vector.tensor_tensor(m, (psA, psB)[u % 2][:, :], m, ALU.add).then_inc(s_pre, 1)
                        if not first:
                            third_part(g - 1, before)
                        nc.vector.tensor_tensor(onehot[:, u % 2, :, :],
                                                iota[:, 0:WIN].unsqueeze(1).to_broadcast([P, TILES, WIN]),
                                                dstT[:, bass.ds(g, 1), :].rearrange("p a j -> p j a").to_broadcast([P, TILES, WIN]),
                                                ALU.is_equal).then_inc(s_onehot, 1)
                        dve.wait_ge(s_part0, layer * GROUPS + g + 1)
                        nc.vector.scalar_tensor_tensor(m, m, 0.0, parts[:, u % 2, 0, :, :].rearrange("p j f -> p (j f)"), ALU.max, ALU.subtract).then_inc(s_rest, 1)
                        if not first:
                            accumulate(g - 1, before, base_before)

                    bases = load_bases(0, SLOTS)
                    for u in range(SLOTS):
                        step(0, u, bases[u], bases[u - 1], first=(u == 0))
                    with dve.Fori(1, ITERS) as it:
                        bases = load_bases(it * SLOTS - 1, SLOTS + 1)
                        for u in range(SLOTS):
                            step(it, u, bases[u + 1], bases[u])
                    third_part(GROUPS - 1, SLOTS - 1)
                    base = load_bases(GROUPS - 1, 1)[0]
                    accumulate(GROUPS - 1, SLOTS - 1, base)

            with nc.If(far > 0):
                with nc.Block() as block:
                    @block.sync
                    def _(sp):
                        def load(n, start, edges=GROUP):
                            sp.wait_ge(f_scatter, (layer * GROUPS + n) * CHUNKS + 1)
                            sp.dma_start(attr[0:edges // TILES, 0, :], edge_attr[bass.ds(start, edges), :].rearrange("(p j) k -> p (j k)", j=TILES)).then_inc(f_attr, 16)
                        with sp.Fori(0, GROUPS - 2) as g:
                            load(g, g * GROUP)
                        load(GROUPS - 2, (GROUPS - 2) * GROUP, REST)
                        load(GROUPS - 1, N_EDGES - GROUP)

                    @block.gpsimd
                    def _(pool):
                        with pool.Fori(0, GROUPS) as g:
                            hold(pool, f_idx, layer * GROUPS + g + 1)
                            for j in range(TILES):
                                nc.gpsimd.indirect_dma_start(msg[:, 0, j, :], None, gather_rows[0:N_NODES, :],
                                                             bass.IndirectOffsetOnAxis(ap=idx[0][:, j:j + 1], axis=0)).then_inc(f_gather, 16)

                    @block.scalar
                    def _(act):
                        with act.Fori(0, GROUPS) as g:
                            n = layer * GROUPS + g + 1
                            hold(act, f_scatter, (n - 1) * CHUNKS + 1)
                            nc.scalar.activation(idx[0][:, :], srcT[:, bass.ds(g, 1), :].rearrange("p a j -> p (a j)"), ACT.Copy).then_inc(f_idx, 1)
                            act.wait_ge(f_attrT, n)
                            nc.scalar.activation(attrT[:, 0, :], psC[0:TILES * DE, 0:P], ACT.Copy).then_inc(f_attrT_sb, 1)
                            act.wait_ge(f_pre, n)
                            nc.scalar.activation(msg[:, 0, :, :], msg[:, 0, :, :], ACT.Relu).then_inc(f_relu, 1)

                    @block.tensor
                    def _(pe):
                        with pe.Fori(0, GROUPS) as g:
                            n = layer * GROUPS + g + 1
                            hold(pe, f_attr, n * 16)
                            nc.tensor.transpose(psC[0:TILES * DE, 0:P], attr[:, 0, :], ident[:, :]).then_inc(f_attrT, 1)
                            pe.wait_ge(f_attrT_sb, n)
                            nc.tensor.matmul(psA[:, :], attrT[:, 0, :], w1e[:, :, :].rearrange("p j f -> p (j f)"), start=True, stop=True).then_inc(f_term, 1)
                            hold(pe, f_relu, n)
                            with pe.Fori(0, CHUNKS) as c:
                                hold(pe, f_onehot, (n - 1) * CHUNKS + c + 1)
                                for j in range(TILES):
                                    nc.tensor.matmul(psE[:, :], msg[:, 0, j, :], wide[:, j, :], start=(j == 0), stop=(j == TILES - 1))
                                for j in range(TILES):
                                    last = nc.tensor.matmul(psF[:, :], ones[:, :], wide[:, j, :], start=(j == 0), stop=(j == TILES - 1))
                                last.then_inc(f_scatter, 1)

                    @block.vector
                    def _(dve):
                        with dve.Fori(0, GROUPS) as g:
                            n = layer * GROUPS + g + 1
                            dve.wait_ge(f_gather, n * 64)
                            dve.wait_ge(f_term, n)
                            m = msg[:, 0, :, :].rearrange("p j f -> p (j f)")
                            nc.vector.tensor_tensor(m, psA[:, :], m, ALU.add).then_inc(f_pre, 1)
                            with dve.Fori(0, CHUNKS) as c:
                                link = Chain(dve, f_rel, (n - 1) * CHUNKS + c)
                                link.link(nc.vector.tensor_tensor(rel[:, :], far_dst[:, bass.ds(g, 1), :].rearrange("p a j -> p (a j)"),
                                                                  chunk_start[:, bass.ds(c, 1)].to_broadcast([P, TILES]), ALU.subtract))
                                nc.vector.tensor_tensor(wide[:, :, :], iota[:, :].unsqueeze(1).to_broadcast([P, TILES, CHUNK]),
                                                        rel[:, :].unsqueeze(2).to_broadcast([P, TILES, CHUNK]), ALU.is_equal).then_inc(f_onehot, 1)
                                hold(dve, f_scatter, (n - 1) * CHUNKS + c + 2)
                                a0, a1 = acc[:, 0, bass.ds(c * CHUNK, CHUNK)], acc[:, 1, bass.ds(c * CHUNK, CHUNK)]
                                nc.vector.tensor_tensor(a0, a0, psE[:, :], ALU.add)
                                nc.vector.tensor_tensor(a1, a1, psF[:, :], ALU.add)

            with nc.Block() as block:
                @block.sync
                def _(sp):
                    sp.dma_start(w2[:, :], W2[bass.ds(layer, 1), :, :].rearrange("a k f -> (a k) f")).then_inc(s_nw, 16)
                    sp.dma_start(wself[:, :], Wself[bass.ds(layer, 1), :, :].rearrange("a k f -> (a k) f")).then_inc(s_nw, 16)
                    sp.dma_start(b2_row[:, :], b2[bass.ds(layer, 1), :]).then_inc(s_nw, 16)
                    sp.dma_start(bself_col[:, :], bself[bass.ds(layer, 1), :].rearrange("a (p b) -> (a p) b", b=1)).then_inc(s_nw, 16)
                    nxt = (layer + 1) % N_LAYERS
                    sp.dma_start(w1x[:, :], W1[bass.ds(nxt, 1), 0:D, :].rearrange("a k f -> (a k) f")).then_inc(s_nw, 16)
                    sp.dma_start(b1_row[:, :], b1[bass.ds(nxt, 1), :]).then_inc(s_nw, 16)
                    hold(sp, s_nw, (layer + 1) * 96)
                    with sp.Fori(0, CHUNKS) as c:
                        sp.wait_ge(s_rows_sb, layer * CHUNKS + c + 1)
                        sp.dma_start(gather_rows[bass.ds(c * CHUNK, CHUNK), :].rearrange("(s p) f -> p s f", p=P), rows_out[:, :, :]).then_inc(s_rows_st, 16)
                    hold(sp, s_rows_st, (layer + 1) * CHUNKS * 16)

                @block.vector
                def _(dve):
                    with dve.Fori(0, CHUNKS) as c:
                        n = layer * CHUNKS + c + 1
                        total, count = acc[:, 0, bass.ds(c * CHUNK, CHUNK)], acc[:, 1, bass.ds(c * CHUNK, CHUNK)]
                        chain = Chain(dve, s_node_chain, (n - 1) * 2)
                        chain.link(nc.vector.tensor_scalar(stage2[:, :], count, 1.0, None, ALU.max))
                        chain.link(nc.vector.reciprocal(stage2[:, :], stage2[:, :]))
                        nc.vector.tensor_tensor(ind[:, :], count, stage2[:, :], ALU.mult)
                        nc.vector.tensor_tensor(stage[:, :], total, stage2[:, :], ALU.mult).then_inc(s_mean, 1)
                        dve.wait_ge(s_rows_ps, n)
                        nc.vector.tensor_copy(rows_out[:, :, :], psB[:, :].rearrange("p (s f) -> p s f", s=TILES)).then_inc(s_rows_sb, 1)
                        nc.vector.tensor_copy(acc[:, :, bass.ds(c * CHUNK, CHUNK)], zero_col[:, :].unsqueeze(1).to_broadcast([P, 2, CHUNK]))
                        hold(dve, s_rows_st, n * 16)

                @block.tensor
                def _(pe):
                    hold(pe, s_nw, (layer + 1) * 96)
                    with pe.Fori(0, CHUNKS) as c:
                        n = layer * CHUNKS + c + 1
                        pe.wait_ge(s_mean, n)
                        nc.tensor.matmul(psA[:, :], w2[:, :], stage[:, :], start=True, stop=False)
                        nc.tensor.matmul(psA[:, :], b2_row[:, :], ind[0:1, :], start=False, stop=False)
                        nc.tensor.matmul(psA[:, :], wself[:, :], nodeT[:, bass.ds(c * CHUNK, CHUNK)], start=False, stop=True).then_inc(s_x_ps, 1)
                        pe.wait_ge(s_x_sb, n)
                        for s in range(TILES):
                            nc.tensor.matmul(psB[:, s * D:(s + 1) * D], x_stage[:, s * P:(s + 1) * P], w1x[:, :], start=True, stop=False)
                            last = nc.tensor.matmul(psB[:, s * D:(s + 1) * D], ones[0:1, :], b1_row[:, :], start=False, stop=True)
                        last.then_inc(s_rows_ps, 1)

                @block.scalar
                def _(act):
                    hold(act, s_nw, (layer + 1) * 96)
                    with act.Fori(0, CHUNKS) as c:
                        hold(act, s_x_ps, layer * CHUNKS + c + 1)
                        nc.scalar.activation(nodeT[:, bass.ds(c * CHUNK, CHUNK)], psA[:, :], ACT.Identity, bias=bself_col[:, :])
                        nc.scalar.activation(x_stage[:, :], psA[:, :], ACT.Identity, bias=bself_col[:, :]).then_inc(s_x_sb, 1)

        def layernorm(dve, chain, n, y, result, signal):
            chain.link(nc.vector.bn_stats(stats[:, :], y), held=True)
            nc.vector.bn_aggr(mv[:, :], stats[:, :]).then_inc(s_var, 1)
            dve.wait_ge(s_std, n)
            chain.link(nc.vector.reciprocal(rstd[:, :], std[:, :]))
            nc.vector.tensor_scalar(result, y, mv[:, 0:1], rstd[:, :], ALU.subtract, ALU.mult).then_inc(signal, 1)

        def root(act, n):
            act.wait_ge(s_var, n)
            nc.scalar.activation(std[:, :], mv[:, 1:2], ACT.Sqrt, bias=eps_col[:, :]).then_inc(s_std, 1)

        with nc.Block() as block:
            @block.sync
            def _(sp):
                def tile(t, rows):
                    sp.dma_start(rows_in[0:rows, 0, :], x[bass.ds(t * P, rows), :]).then_inc(s_x_in, 16)
                    sp.wait_ge(s_z, t + 1)
                    sp.dma_start(z_rows[bass.ds(t * P, P), :], z_out[:, :]).then_inc(s_z_st, 16)
                    sp.wait_ge(s_kv_sb, t + 1)
                    sp.dma_start(kv_rows[bass.ds(t * P, P), :], kv_out[:, :]).then_inc(s_kv_st, 16)
                with sp.Fori(0, NTILES - 1) as t:
                    tile(t, P)
                tile(NTILES - 1, LAST_ROWS)
                sp.wait_ge(s_z_st, NTILES * 16)
                sp.wait_ge(s_kv_st, NTILES * 16)

            @block.scalar
            def _(act):
                nc.scalar.mul(tau_bq[:, :], bq_col[:, :], TAU).then_inc(s_tau_bq, 1)
                act.wait_ge(s_tau_bq, 1)
                with act.Fori(0, NTILES) as t:
                    nc.scalar.activation(x_stage[:, 0:P], nodeT[:, bass.ds(t * P, P)], ACT.Copy).then_inc(s_xs, 1)
                    root(act, t + 1)
                    act.wait_ge(s_zT_ps, t + 1)
                    nc.scalar.activation(zT[:, :], psC[:, 0:P], ACT.Copy).then_inc(s_zT, 1)
                    hold(act, s_q_ps, t + 1)
                    nc.scalar.activation(nodeT[:, bass.ds(t * P, P)], psD[:, 0:P], ACT.Identity, bias=tau_bq[:, :], scale=TAU)

            @block.tensor
            def _(pe):
                with pe.Fori(0, NTILES) as t:
                    pe.wait_ge(s_xs, t + 1)
                    nc.tensor.transpose(psA[:, 0:P], x_stage[:, 0:P], ident[:, :]).then_inc(s_x3, 1)
                    pe.wait_ge(s_z, t + 1)
                    nc.tensor.transpose(psC[:, 0:P], z_out[:, :], ident[:, :]).then_inc(s_zT_ps, 1)
                    pe.wait_ge(s_zT, t + 1)
                    nc.tensor.matmul(psD[:, 0:P], wq[:, :], zT[:, :], start=True, stop=True).then_inc(s_q_ps, 1)
                    nc.tensor.matmul(psB[:, 0:2 * D], zT[:, :], wkv[:, :], start=True, stop=False)
                    nc.tensor.matmul(psB[:, 0:2 * D], ones[0:1, :], bkv_row[:, :], start=False, stop=True).then_inc(s_kv_ps, 1)

            @block.vector
            def _(dve):
                nc.vector.memset(maxB[:, :], NO_MAX)
                with dve.Fori(0, NTILES) as t:
                    dve.wait_ge(s_x_in, (t + 1) * 16)
                    dve.wait_ge(s_x3, t + 1)
                    chain = Chain(dve, s_z_chain, t * 6)
                    chain.link(nc.vector.tensor_tensor(rows_out[:, 3, :], psA[:, 0:P], rows_in[:, 0, :], ALU.add))
                    layernorm(dve, chain, t + 1, rows_out[:, 3, :], z_out[:, :], s_z)
                    dve.wait_ge(s_kv_ps, t + 1)
                    v = kv_out[:, D:KV].bitcast(bf16).rearrange("p (k f) -> p k f", k=3)
                    nc.vector.tensor_copy(kv_out[:, 0:D], psB[:, 0:D])
                    chain.link(nc.vector.tensor_copy(v[:, 0, :], psB[:, D:2 * D]))
                    chain.link(nc.vector.tensor_tensor(rows_out[:, 0, :], psB[:, D:2 * D], v[:, 0, :], ALU.subtract))
                    chain.link(nc.vector.tensor_copy(v[:, 1, :], rows_out[:, 0, :]))
                    nc.vector.tensor_tensor(v[:, 2, :], rows_out[:, 0, :], v[:, 1, :], ALU.subtract).then_inc(s_kv_sb, 1)
                    dve.wait_ge(s_kv_st, (t + 1) * 16)
                    hold(dve, s_z_st, (t + 1) * 16)

        with nc.Block() as block:
            @block.gpsimd
            def _(pool):
                with pool.Fori(0, ITERS) as it:
                    for u in range(SLOTS):
                        hold(pool, s_idx, N_LAYERS * GROUPS + it * SLOTS + u + 1)
                        for j in range(TILES):
                            nc.gpsimd.indirect_dma_start(kv[:, u, j, :], None, kv_rows[0:N_NODES, :],
                                                         bass.IndirectOffsetOnAxis(ap=idx[u][:, j:j + 1], axis=0)).then_inc(s_gather[u], 16)

            @block.scalar
            def _(act):
                def copy_idx(g, u):
                    hold(act, s_slot_free, N_LAYERS * GROUPS + g + 1)
                    nc.scalar.activation(idx[u][:, :], srcT[:, bass.ds(g, 1), :].rearrange("p a j -> p (a j)"), ACT.Copy).then_inc(s_idx, 1)

                def keys(g):
                    act.wait_ge(s_keysT_ps, 2 * g + 1)
                    nc.scalar.activation(keysT[:, 0:2 * P], psA[:, 0:2 * P], ACT.Copy).then_inc(s_keysT, 1)
                    act.wait_ge(s_keysT_ps, 2 * g + 2)
                    nc.scalar.activation(keysT[:, 2 * P:4 * P], psG[:, 0:2 * P], ACT.Copy).then_inc(s_keysT, 1)

                def terms(g, u):
                    k = u % 2
                    act.wait_ge(s_shifted, g + 1)
                    nc.scalar.activation(score[:, k, :, :], score[:, k, :, :], ACT.Exp).then_inc(s_probs, 1)
                    nc.scalar.activation(decay[:, k, :], decay[:, k, :], ACT.Exp)
                    act.wait_ge(s_probs, g + 1)
                    nc.scalar.activation(probs[:, k, 0, :, :], score[:, k, :, :], ACT.Copy).then_inc(s_prob0, 1)
                    act.wait_ge(s_prob_rest, g + 1)
                    nc.scalar.activation(probs[:, k, 1, :, :], score[:, k, :, :], ACT.Copy).then_inc(s_prob1, 1)

                for u in range(SLOTS - 1):
                    copy_idx(u, u)
                keys(0)
                keys(1)
                with act.Fori(0, ITERS - 1) as it:
                    for u in range(SLOTS):
                        g = it * SLOTS + u
                        terms(g, u)
                        keys(g + 2)
                        copy_idx(g + SLOTS - 1, (u + SLOTS - 1) % SLOTS)
                for u in range(SLOTS):
                    g = GROUPS - SLOTS + u
                    terms(g, u)
                    if u + 2 < SLOTS:
                        keys(g + 2)
                    if u == 0:
                        copy_idx(g + SLOTS - 1, SLOTS - 1)

            @block.tensor
            def _(pe):
                regs = [nc.tensor.alloc_register(f"pbase{u}") for u in range(SLOTS + 1)]

                def load_bases(first):
                    nc.tensor.load(regs, base_row[0:1, bass.ds(first, SLOTS + 1)])
                    return [nc.tensor.snap(r, min_val=0, max_val=PAD_DST) for r in regs]

                def keys(g, u, it):
                    hold(pe, s_gather[u], (N_LAYERS * ITERS + it + 1) * 64)
                    for j in range(TILES):
                        last = nc.tensor.transpose((psA, psG)[j // 2][:, (j % 2) * P:(j % 2 + 1) * P], kv[:, u, j, 0:D], ident[:, :])
                        if j % 2:
                            last.then_inc(s_keysT_ps, 1)

                def scores(g, base):
                    for j in range(TILES):
                        if j % 2 == 0:
                            hold(pe, s_keysT, 2 * g + 1 + j // 2)
                        last = nc.tensor.matmul(psB[:, j * WIN:(j + 1) * WIN], keysT[:, j * P:(j + 1) * P], nodeT[:, bass.ds(base, WIN)], start=True, stop=True)
                    last.then_inc(s_score_ps, 1)

                def scores_transposed(g, u):
                    hold(pe, s_masked, g + 1)
                    nc.tensor.transpose(psC[:, 0:P], score[:, u % 2, :, :].rearrange("p j w -> p (j w)"), ident[:, :]).then_inc(s_scoreT, 1)

                def spread_max(g):
                    hold(pe, s_diag, g + 1)
                    nc.tensor.matmul(psD[:, 0:P], ones[:, :], diag[:, :], start=True, stop=True).then_inc(s_maxB_ps, 1)

                def mix(g, u, first=False):
                    v = kv[:, u, :, D:KV].bitcast(bf16)
                    p = probs[:, u % 2, :, :, :]
                    if not first:
                        hold(pe, s_slot_free, N_LAYERS * GROUPS + SLOTS + g)
                    hold(pe, s_terms, g + 1)
                    pairs = [(a, b) for a in range(3) for b in range(3) if a + b < 3]
                    for i, (a, b) in enumerate(pairs):
                        for j in range(TILES):
                            nc.tensor.matmul(psE[:, 0:WIN], v[:, j, a * D:(a + 1) * D], p[:, b, j, :],
                                             start=(i + j == 0), stop=(i == len(pairs) - 1 and j == TILES - 1))
                    for b in range(3):
                        last = nc.tensor.matmul(psF[:, 0:P], ones_h[:, :], p[:, b, :, :].rearrange("p j w -> p (j w)"), start=(b == 0), stop=(b == 2))
                    last.then_inc(s_mix, 1)

                def step(it, u, base_next, first=False, last=SLOTS):
                    g = it * SLOTS + u
                    spread_max(g)
                    if u + 1 < last:
                        scores(g + 1, base_next)
                    if not (first and u == 0):
                        mix(g - 1, (u - 1) % SLOTS, first=first and u == 1)
                    if u + 1 < last:
                        scores_transposed(g + 1, u + 1)
                    if u + 2 < last:
                        keys(g + 2, (u + 2) % SLOTS, it + (u + 2) // SLOTS)

                bases = load_bases(0)
                keys(0, 0, 0)
                scores(0, bases[0])
                scores_transposed(0, 0)
                keys(1, 1, 0)
                for u in range(SLOTS):
                    step(0, u, bases[u + 1], first=True, last=SLOTS + 2)
                with pe.Fori(1, ITERS - 1) as it:
                    bases = load_bases(it * SLOTS)
                    for u in range(SLOTS):
                        step(it, u, bases[u + 1], last=SLOTS + 2)
                bases = load_bases(GROUPS - SLOTS)
                for u in range(SLOTS):
                    step(ITERS - 1, u, bases[u + 1])
                mix(GROUPS - 1, SLOTS - 1)

            @block.vector
            def _(dve):
                regs = [nc.vector.alloc_register(f"abase{u}") for u in range(SLOTS + 1)]

                def load_bases(first, count=SLOTS + 1):
                    nc.vector.load(regs[0:count], base_row[0:1, bass.ds(first, count)])
                    return [nc.vector.snap(r, min_val=0, max_val=PAD_DST) for r in regs[0:count]]

                def find_outside(g, u):
                    nc.vector.tensor_tensor(outside[:, u % 2, :, :],
                                            iota[:, 0:WIN].unsqueeze(1).to_broadcast([P, TILES, WIN]),
                                            dstT[:, bass.ds(g, 1), :].rearrange("p a j -> p j a").to_broadcast([P, TILES, WIN]),
                                            ALU.not_equal).then_inc(s_outside, 1)

                def mask(g, u):
                    dve.wait_ge(s_outside, g + 1)
                    dve.wait_ge(s_score_ps, g + 1)
                    nc.vector.scalar_tensor_tensor(score[:, u % 2, :, :].rearrange("p j w -> p (j w)"), outside[:, u % 2, :, :].rearrange("p j w -> p (j w)"),
                                                   MASKED, psB[:, 0:P], ALU.mult, ALU.add).then_inc(s_masked, 1)

                def group_maxima(g, base_before=None):
                    dve.wait_ge(s_scoreT, g + 1)
                    nc.vector.reduce_max(gmax[:, :], psC[:, 0:P], AX.X).then_inc(s_gmax, 1)
                    if base_before is not None:
                        nc.vector.tensor_copy(maxB[:, bass.ds(base_before, WIN)], new_max[:, :])
                    dve.wait_ge(s_gmax, g + 1)
                    nc.vector.tensor_scalar(diag[:, :], ident[:, :], gmax[:, :], None, ALU.mult).then_inc(s_diag, 1)

                def shift(g, u, base, chain):
                    win = maxB[:, bass.ds(base, WIN)]
                    dve.wait_ge(s_maxB_ps, g + 1)
                    chain.link(nc.vector.reduce_max(group_max[:, :], psD[:, 0:P].rearrange("p (j w) -> p w j", j=TILES), AX.X))
                    chain.link(nc.vector.tensor_tensor(new_max[:, :], group_max[:, :], win, ALU.max))
                    nc.vector.tensor_tensor(decay[:, u % 2, :], win, new_max[:, :], ALU.subtract)
                    nc.vector.tensor_tensor(score[:, u % 2, :, :], score[:, u % 2, :, :], new_max[:, :].unsqueeze(1).to_broadcast([P, TILES, WIN]), ALU.subtract).then_inc(s_shifted, 1)

                def rest_of_terms(g, u):
                    dve.wait_ge(s_prob0, g + 1)
                    nc.vector.tensor_tensor(score[:, u % 2, :, :], score[:, u % 2, :, :], probs[:, u % 2, 0, :, :], ALU.subtract).then_inc(s_prob_rest, 1)

                def third_part(g, u):
                    dve.wait_ge(s_prob1, g + 1)
                    nc.vector.tensor_tensor(probs[:, u % 2, 2, :, :], score[:, u % 2, :, :], probs[:, u % 2, 1, :, :], ALU.subtract).then_inc(s_terms, 1)

                def accumulate(g, u, base, chain):
                    dve.wait_ge(s_mix, g + 1)
                    a, a0, a1 = acc[:, :, bass.ds(base, WIN)], acc[:, 0, bass.ds(base, WIN)], acc[:, 1, bass.ds(base, WIN)]
                    nc.vector.tensor_tensor(a, a, decay[:, u % 2, :].unsqueeze(1).to_broadcast([P, 2, WIN]), ALU.mult)
                    chain.link(nc.vector.tensor_reduce(group_den[:, :], psF[:, 0:P].rearrange("p (j w) -> p w j", j=TILES), AX.X, ALU.add))
                    nc.vector.tensor_tensor(a1, a1, group_den[:, :], ALU.add)
                    nc.vector.tensor_tensor(a0, a0, psE[:, 0:WIN], ALU.add).then_inc(s_slot_free, 1)

                def step(it, u, base, base_before, first=False, last=SLOTS):
                    g = it * SLOTS + u
                    shift(g, u, base, Chain(dve, s_attn_chain, g * 2))
                    rest_of_terms(g, u)
                    if u + 1 < last:
                        mask(g + 1, u + 1)
                    third_part(g, u)
                    if u + 2 < last:
                        find_outside(g + 2, u + 2)
                    if u + 1 < last:
                        group_maxima(g + 1, base)
                    if not (first and u == 0):
                        accumulate(g - 1, (u - 1) % SLOTS, base_before, Chain(dve, s_den_chain, g - 1))

                bases = load_bases(0)
                find_outside(0, 0)
                mask(0, 0)
                find_outside(1, 1)
                group_maxima(0)
                for u in range(SLOTS):
                    step(0, u, bases[u], bases[u - 1], first=True, last=SLOTS + 2)
                with dve.Fori(1, ITERS - 1) as it:
                    bases = load_bases(it * SLOTS - 1)
                    for u in range(SLOTS):
                        step(it, u, bases[u + 1], bases[u], last=SLOTS + 2)
                bases = load_bases(GROUPS - SLOTS - 1)
                for u in range(SLOTS):
                    step(ITERS - 1, u, bases[u + 1], bases[u])
                nc.vector.tensor_copy(maxB[:, bass.ds(bases[SLOTS], WIN)], new_max[:, :])
                accumulate(GROUPS - 1, SLOTS - 1, bases[SLOTS], Chain(dve, s_den_chain, GROUPS - 1))

        with nc.If(far > 0):
            with nc.Block() as block:
                @block.sync
                def _(sp):
                    sp.wait_ge(h_mix, GROUPS * TILES * CHUNKS + 1)

                @block.gpsimd
                def _(pool):
                    with pool.Fori(0, GROUPS) as g:
                        hold(pool, h_idx, g + 1)
                        for j in range(TILES):
                            nc.gpsimd.indirect_dma_start(kv[:, 0, j, :], None, kv_rows[0:N_NODES, :],
                                                         bass.IndirectOffsetOnAxis(ap=idx[0][:, j:j + 1], axis=0)).then_inc(h_gather, 16)

                @block.scalar
                def _(act):
                    with act.Fori(0, GROUPS) as g:
                        hold(act, h_mix, g * TILES * CHUNKS + 1)
                        nc.scalar.activation(idx[0][:, :], srcT[:, bass.ds(g, 1), :].rearrange("p a j -> p (a j)"), ACT.Copy).then_inc(h_idx, 1)
                        act.wait_ge(h_keysT_ps, g + 1)
                        nc.scalar.activation(keysT[:, :], psA[:, :], ACT.Copy).then_inc(h_keysT, 1)
                        for j in range(TILES):
                            with act.Fori(0, CHUNKS) as c:
                                act.wait_ge(h_shifted, (g * TILES + j) * CHUNKS + c + 1)
                                nc.scalar.activation(wide[:, 2, :], wide[:, 2, :], ACT.Exp)
                                nc.scalar.activation(wide[:, 0, :], wide[:, 0, :], ACT.Exp).then_inc(h_probs, 1)

                @block.tensor
                def _(pe):
                    with pe.Fori(0, GROUPS) as g:
                        hold(pe, h_gather, (g + 1) * 64)
                        for j in range(TILES):
                            last = nc.tensor.transpose(psA[:, j * P:(j + 1) * P], kv[:, 0, j, 0:D], ident[:, :])
                        last.then_inc(h_keysT_ps, 1)
                        hold(pe, h_keysT, g + 1)
                        for j in range(TILES):
                            with pe.Fori(0, CHUNKS) as c:
                                m = (g * TILES + j) * CHUNKS + c + 1
                                nc.tensor.matmul(psB[:, :], keysT[:, j * P:(j + 1) * P], nodeT[:, bass.ds(c * CHUNK, CHUNK)], start=True, stop=True).then_inc(h_score, 1)
                                hold(pe, h_masked, m)
                                for b in range(TILES):
                                    last = nc.tensor.transpose(psC[:, b * P:(b + 1) * P], wide[:, 0, b * P:(b + 1) * P], ident[:, :])
                                last.then_inc(h_scoreT, 1)
                                hold(pe, h_diag, m)
                                nc.tensor.matmul(psD[:, :], ones[:, :], stage[:, :], start=True, stop=True).then_inc(h_max, 1)
                                hold(pe, h_probs, m)
                                nc.tensor.matmul(psE[:, :], rows_out[:, j, :], wide[:, 0, :], start=True, stop=True)
                                nc.tensor.matmul(psF[:, :], ones[:, :], wide[:, 0, :], start=True, stop=True).then_inc(h_mix, 1)

                @block.vector
                def _(dve):
                    with dve.Fori(0, GROUPS) as g:
                        dve.wait_ge(h_gather, (g + 1) * 64)
                        v = kv[:, 0, :, D:KV].bitcast(bf16)
                        link = Chain(dve, h_value, g * 2)
                        link.link(nc.vector.tensor_tensor(rows_out[:, :, :], v[:, :, D:2 * D], v[:, :, 2 * D:3 * D], ALU.add))
                        link.link(nc.vector.tensor_tensor(rows_out[:, :, :], rows_out[:, :, :], v[:, :, 0:D], ALU.add), held=True)
                        for j in range(TILES):
                            with dve.Fori(0, CHUNKS) as c:
                                m = (g * TILES + j) * CHUNKS + c + 1
                                chain = Chain(dve, h_chain, (m - 1) * 5)
                                chain.link(nc.vector.tensor_tensor(rel[:, 0:1], far_dst[:, bass.ds(g, 1), j], chunk_start[:, bass.ds(c, 1)], ALU.subtract))
                                chain.link(nc.vector.tensor_tensor(wide[:, 1, :], iota[:, :], rel[:, 0:1].to_broadcast([P, CHUNK]), ALU.not_equal))
                                dve.wait_ge(h_score, m)
                                nc.vector.scalar_tensor_tensor(wide[:, 0, :], wide[:, 1, :], MASKED, psB[:, :], ALU.mult, ALU.add).then_inc(h_masked, 1)
                                dve.wait_ge(h_scoreT, m)
                                chain.link(nc.vector.reduce_max(gmax4[:, :], psC[:, :].rearrange("p (b e) -> p b e", b=TILES), AX.X))
                                nc.vector.tensor_tensor(stage[:, :].rearrange("p (b w) -> p b w", b=TILES), ident[:, :].unsqueeze(1).to_broadcast([P, TILES, P]),
                                                        gmax4[:, :].unsqueeze(2).to_broadcast([P, TILES, P]), ALU.mult).then_inc(h_diag, 1)
                                dve.wait_ge(h_max, m)
                                win = maxB[:, bass.ds(c * CHUNK, CHUNK)]
                                chain.link(nc.vector.tensor_tensor(wide[:, 3, :], psD[:, :], win, ALU.max))
                                nc.vector.tensor_tensor(wide[:, 2, :], win, wide[:, 3, :], ALU.subtract)
                                nc.vector.tensor_tensor(wide[:, 0, :], wide[:, 0, :], wide[:, 3, :], ALU.subtract).then_inc(h_shifted, 1)
                                dve.wait_ge(h_mix, m + 1)
                                a = acc[:, :, bass.ds(c * CHUNK, CHUNK)]
                                nc.vector.tensor_tensor(a, a, wide[:, 2, :].unsqueeze(1).to_broadcast([P, 2, CHUNK]), ALU.mult)
                                chain.link(nc.vector.tensor_copy(win, wide[:, 3, :]))
                                a0, a1 = acc[:, 0, bass.ds(c * CHUNK, CHUNK)], acc[:, 1, bass.ds(c * CHUNK, CHUNK)]
                                nc.vector.tensor_tensor(a0, a0, psE[:, :], ALU.add)
                                nc.vector.tensor_tensor(a1, a1, psF[:, :], ALU.add)

        with nc.Block() as block:
            @block.sync
            def _(sp):
                def tile(t, rows):
                    sp.dma_start(rows_in[:, 0, :], z_rows[bass.ds(t * P, P), :]).then_inc(s_z_in, 16)
                    sp.wait_ge(s_o, t + 1)
                    sp.dma_start(out[bass.ds(t * P, rows), :], z_out[0:rows, :]).then_inc(s_out, 16)
                with sp.Fori(0, NTILES - 1) as t:
                    tile(t, P)
                tile(NTILES - 1, LAST_ROWS)
                sp.wait_ge(s_out, NTILES * 16)

            @block.scalar
            def _(act):
                with act.Fori(0, NTILES) as t:
                    root(act, t + 1 + NTILES)

            @block.tensor
            def _(pe):
                with pe.Fori(0, NTILES) as t:
                    pe.wait_ge(s_h, t + 1)
                    nc.tensor.transpose(psA[:, 0:P], stage[:, 0:P], ident[:, :]).then_inc(s_hT, 1)

            @block.vector
            def _(dve):
                with dve.Fori(0, NTILES) as t:
                    den = acc[:, 1, bass.ds(t * P, P)]
                    chain = Chain(dve, s_out_chain, t * 5)
                    chain.link(nc.vector.scalar_tensor_tensor(stage2[:, 0:P], den, 0.0, den, ALU.is_equal, ALU.add))
                    chain.link(nc.vector.reciprocal(stage2[:, 0:P], stage2[:, 0:P]))
                    nc.vector.tensor_tensor(stage[:, 0:P], acc[:, 0, bass.ds(t * P, P)], stage2[:, 0:P], ALU.mult).then_inc(s_h, 1)
                    dve.wait_ge(s_z_in, (t + 1) * 16)
                    dve.wait_ge(s_hT, t + 1)
                    chain.link(nc.vector.tensor_tensor(rows_out[:, 3, :], psA[:, 0:P], rows_in[:, 0, :], ALU.add))
                    layernorm(dve, chain, t + 1 + NTILES, rows_out[:, 3, :], z_out[:, :], s_o)
                    hold(dve, s_out, (t + 1) * 16)



def kernel(**inputs):
    import numpy as _np
    import concourse.bacc as _bacc
    from concourse import mybir as _mybir
    from concourse.bass_utils import run_bass_kernel_spmd as _run
    nc = _bacc.Bacc("TRN2", target_bir_lowering=False, num_devices=1)
    names = ["x", "src", "dst", "edge_attr_16", "L0_gnn_W1", "L0_gnn_b1", "L0_gnn_W2", "L0_gnn_b2", "L0_gnn_Wself", "L0_gnn_bself",
             "L1_gnn_Wq", "L1_gnn_bq", "L1_gnn_Wk", "L1_gnn_bk", "L1_gnn_Wv", "L1_gnn_bv"]
    arrays, args = {}, []
    for name in names:
        a = _np.ascontiguousarray(inputs[name])
        arrays[f"in_{name}"] = a
        args.append(nc.dram_tensor(f"in_{name}", a.shape, _mybir.dt.from_np(a.dtype), kind="ExternalInput").ap())
    out = nc.dram_tensor("out", (N_NODES, D), _mybir.dt.float32, kind="ExternalOutput").ap()
    gnn_attention(nc, *args, out)
    r = _run(nc, [arrays], core_ids=[0])
    return r.results[0]["out"]
```
